# Optimizing a Trainium2 kernel written in Bass

```python
import numpy as np
import jax
import jax.numpy as jnp

def _softmax(x, axis=-1):
    return jax.nn.softmax(x, axis=axis)

def _gelu(x):
    return jax.nn.gelu(x, approximate=True)

def _silu(x):
    return jax.nn.silu(x)

def _sigmoid(x):
    return jax.nn.sigmoid(x)

def _layernorm(x, axis=-1, eps=1e-05):
    m = jnp.mean(x, axis=axis, keepdims=True)
    v = jnp.var(x, axis=axis, keepdims=True)
    return (x - m) / jnp.sqrt(v + eps)

def _scatter_add(tgt, idx, src, axis=0):
    return tgt.at[idx].add(src)

def _segment_sum(src, seg, n):
    return jax.ops.segment_sum(src, seg, n)
kernel_name = 'mk_cond_seq_d2_seqx_r2_dd6e07'

def setup_inputs(seed: int=0):
    np.random.seed(seed)
    _w = jnp.asarray

    def _rec_inputs():
        import jax
        import jax.numpy as jnp
        _rk = jax.random.key(seed)
        x = 7.22e-05 + 1 * jax.random.normal(jax.random.fold_in(_rk, 1), (8, 1024, 512), jnp.float32)
        _lenS = 1024 - jax.random.randint(jax.random.fold_in(_rk, 7), (8,), 0, max(1, 1024 // 4) + 1, jnp.int32)
        _lenS2 = 1024 - jax.random.randint(jax.random.fold_in(_rk, 8), (8,), 0, max(1, 1024 // 4) + 1, jnp.int32)
        cond_2048 = 0.00386106 + 1.00199 * jax.random.normal(jax.random.fold_in(_rk, 11), (8, 1024), jnp.float32)
        _validS = jnp.arange(1024)[None, :] < _lenS[:, None]
        _validS2 = jnp.arange(1024)[None, :] < _lenS2[:, None]
        _causal = jnp.tril(jnp.ones((1024, 1024), dtype=bool))
        mask_BxS_ff1 = jnp.where(jnp.ones((8, 1024), dtype=bool), 1.0, 0.0).astype(jnp.float32)
        return (x, cond_2048, mask_BxS_ff1)
    x, cond_2048, mask_BxS_ff1 = _rec_inputs()

    def _L0_cond_setup():
        import jax, jax.numpy as jnp
        import numpy as np
        B, T, D, H, TE = (8, 512, 512, 16, 1024)
        LN_EPS = 1e-05

        def layer_norm(x, w, b):
            m = jnp.mean(x, axis=-1, keepdims=True)
            v = jnp.var(x, axis=-1, keepdims=True)
            return (x - m) / jnp.sqrt(v + LN_EPS) * w + b
        key = jax.random.key(seed)
        ks = jax.random.split(key, 8)
        s = lambda k, sh: jax.random.normal(k, sh, jnp.float32) * 0.02
        return dict(x=jax.random.normal(ks[0], (B, T, D), jnp.float32), emb=jax.random.normal(ks[1], (B, TE), jnp.float32), src_mask=jnp.ones((B, T), jnp.float32), norm_w=jnp.ones((D,), jnp.float32), norm_b=jnp.zeros((D,), jnp.float32), q_w=s(ks[2], (D, D)), q_b=jnp.zeros((D,), jnp.float32), k_w=s(ks[3], (D, D)), k_b=jnp.zeros((D,), jnp.float32), v_w=s(ks[4], (D, D)), v_b=jnp.zeros((D,), jnp.float32), emb_w=s(ks[5], (TE, 2 * D)), emb_b=jnp.zeros((2 * D,), jnp.float32), sb_norm_w=jnp.ones((D,), jnp.float32), sb_norm_b=jnp.zeros((D,), jnp.float32), out_w=s(ks[6], (D, D)), out_b=jnp.zeros((D,), jnp.float32))
    _L0_cond_all = _L0_cond_setup()
    _L0_cond_in = {k: v for k, v in _L0_cond_all.items() if k in ('norm_w', 'norm_b', 'q_w', 'q_b', 'k_w', 'k_b', 'v_w', 'v_b', 'emb_w', 'emb_b', 'sb_norm_w', 'sb_norm_b', 'out_w', 'out_b')}
    del _L0_cond_all

    def _L1_cond_setup():
        import jax, jax.numpy as jnp
        import numpy as np
        D = 512
        DI = 1024
        N = 16
        DT_RANK = 64
        D_CONV = 4
        EPS = 1e-05

        def _layernorm(x, g, b):
            mu = jnp.mean(x, axis=-1, keepdims=True)
            var = jnp.mean((x - mu) ** 2, axis=-1, keepdims=True)
            return (x - mu) * jax.lax.rsqrt(var + EPS) * g + b

        def _mamba(xn, in_proj_w, conv_w, conv_b, x_proj_w, dt_proj_w, dt_proj_b, A_log, D_param, out_proj_w):
            b, sl, _ = xn.shape
            xz = jnp.einsum('bsd,ed->bse', xn, in_proj_w)
            x_in, z = jnp.split(xz, 2, axis=-1)
            xt = jnp.transpose(x_in, (0, 2, 1))
            u = jax.lax.conv_general_dilated(xt, conv_w[:, None, :], (1,), [(D_CONV - 1, 0)], feature_group_count=DI, dimension_numbers=('NCH', 'OIH', 'NCH')) + conv_b[None, :, None]
            u = jax.nn.silu(jnp.transpose(u, (0, 2, 1)))
            x_dbl = jnp.einsum('bsd,ed->bse', u, x_proj_w)
            dt_r, B, C = jnp.split(x_dbl, [DT_RANK, DT_RANK + N], axis=-1)
            dt = jax.nn.softplus(jnp.einsum('bsr,dr->bsd', dt_r, dt_proj_w) + dt_proj_b)
            A = -jnp.exp(A_log)

            def step(h, inp):
                dt_t, B_t, C_t, u_t = inp
                dA = jnp.exp(dt_t[:, :, None] * A)
                h = h * dA + (dt_t * u_t)[:, :, None] * B_t[:, None, :]
                y = jnp.einsum('bdn,bn->bd', h, C_t)
                return (h, y)
            seq = (jnp.transpose(dt, (1, 0, 2)), jnp.transpose(B, (1, 0, 2)), jnp.transpose(C, (1, 0, 2)), jnp.transpose(u, (1, 0, 2)))
            h0 = jnp.zeros((b, DI, N), xn.dtype)
            _, ys = jax.lax.scan(step, h0, seq)
            y = jnp.transpose(ys, (1, 0, 2)) + u * D_param
            y = y * jax.nn.silu(z)
            return jnp.einsum('bsd,ed->bse', y, out_proj_w)
        key = jax.random.key(seed)
        ks = jax.random.split(key, 16)
        s = lambda fan: 1.0 / np.sqrt(fan)
        inp = {'x': jax.random.normal(ks[0], (2, 1024, D), jnp.float32), 'c': jax.random.normal(ks[1], (2, 2 * D), jnp.float32), 'ln_g': jnp.ones((D,), jnp.float32), 'ln_b': jnp.zeros((D,), jnp.float32), 'ada_w': jax.random.normal(ks[2], (3 * D, 2 * D), jnp.float32) * s(2 * D), 'ada_b': jnp.zeros((3 * D,), jnp.float32), 'in_proj_w': jax.random.normal(ks[3], (2 * DI, D), jnp.float32) * s(D), 'conv_w': jax.random.normal(ks[4], (DI, D_CONV), jnp.float32) * s(D_CONV), 'conv_b': jnp.zeros((DI,), jnp.float32), 'x_proj_w': jax.random.normal(ks[5], (DT_RANK + 2 * N, DI), jnp.float32) * s(DI), 'dt_proj_w': jax.random.normal(ks[6], (DI, DT_RANK), jnp.float32) * s(DT_RANK), 'dt_proj_b': jax.random.uniform(ks[7], (DI,), jnp.float32, -4.0, -2.0), 'A_log': jnp.tile(jnp.log(jnp.arange(1, N + 1, dtype=jnp.float32)), (DI, 1)), 'D_param': jnp.ones((DI,), jnp.float32), 'out_proj_w': jax.random.normal(ks[8], (D, DI), jnp.float32) * s(DI)}
        return inp
    _L1_cond_all = _L1_cond_setup()
    _L1_cond_in = {k: v for k, v in _L1_cond_all.items() if k in ('ln_g', 'ln_b', 'ada_w', 'ada_b', 'in_proj_w', 'conv_w', 'conv_b', 'x_proj_w', 'dt_proj_w', 'dt_proj_b', 'A_log', 'D_param', 'out_proj_w')}
    del _L1_cond_all
    return {'x': x, 'cond_2048': cond_2048, 'mask_BxS_ff1': mask_BxS_ff1, 'L0_cond_norm_w': _L0_cond_in['norm_w'], 'L0_cond_norm_b': _L0_cond_in['norm_b'], 'L0_cond_q_w': _L0_cond_in['q_w'], 'L0_cond_q_b': _L0_cond_in['q_b'], 'L0_cond_k_w': _L0_cond_in['k_w'], 'L0_cond_k_b': _L0_cond_in['k_b'], 'L0_cond_v_w': _L0_cond_in['v_w'], 'L0_cond_v_b': _L0_cond_in['v_b'], 'L0_cond_emb_w': _L0_cond_in['emb_w'], 'L0_cond_emb_b': _L0_cond_in['emb_b'], 'L0_cond_sb_norm_w': _L0_cond_in['sb_norm_w'], 'L0_cond_sb_norm_b': _L0_cond_in['sb_norm_b'], 'L0_cond_out_w': _L0_cond_in['out_w'], 'L0_cond_out_b': _L0_cond_in['out_b'], 'L1_cond_ln_g': _L1_cond_in['ln_g'], 'L1_cond_ln_b': _L1_cond_in['ln_b'], 'L1_cond_ada_w': _L1_cond_in['ada_w'], 'L1_cond_ada_b': _L1_cond_in['ada_b'], 'L1_cond_in_proj_w': _L1_cond_in['in_proj_w'], 'L1_cond_conv_w': _L1_cond_in['conv_w'], 'L1_cond_conv_b': _L1_cond_in['conv_b'], 'L1_cond_x_proj_w': _L1_cond_in['x_proj_w'], 'L1_cond_dt_proj_w': _L1_cond_in['dt_proj_w'], 'L1_cond_dt_proj_b': _L1_cond_in['dt_proj_b'], 'L1_cond_A_log': _L1_cond_in['A_log'], 'L1_cond_D_param': _L1_cond_in['D_param'], 'L1_cond_out_proj_w': _L1_cond_in['out_proj_w']}

def reference(x, cond_2048, mask_BxS_ff1, L0_cond_norm_w, L0_cond_norm_b, L0_cond_q_w, L0_cond_q_b, L0_cond_k_w, L0_cond_k_b, L0_cond_v_w, L0_cond_v_b, L0_cond_emb_w, L0_cond_emb_b, L0_cond_sb_norm_w, L0_cond_sb_norm_b, L0_cond_out_w, L0_cond_out_b, L1_cond_ln_g, L1_cond_ln_b, L1_cond_ada_w, L1_cond_ada_b, L1_cond_in_proj_w, L1_cond_conv_w, L1_cond_conv_b, L1_cond_x_proj_w, L1_cond_dt_proj_w, L1_cond_dt_proj_b, L1_cond_A_log, L1_cond_D_param, L1_cond_out_proj_w):
    import jax
    import jax.numpy as jnp

    def _L0_cond_ref(x, emb, src_mask, norm_w, norm_b, q_w, q_b, k_w, k_b, v_w, v_b, emb_w, emb_b, sb_norm_w, sb_norm_b, out_w, out_b):
        import jax, jax.numpy as jnp
        import numpy as np
        B, T, D, H, TE = (8, 512, 512, 16, 1024)
        LN_EPS = 1e-05

        def layer_norm(x, w, b):
            m = jnp.mean(x, axis=-1, keepdims=True)
            v = jnp.var(x, axis=-1, keepdims=True)
            return (x - m) / jnp.sqrt(v + LN_EPS) * w + b
        Bx, Tx, Dx = x.shape
        xn = layer_norm(x, norm_w, norm_b)
        q = (xn @ q_w + q_b).reshape(Bx, Tx, H, -1)
        k = (xn @ k_w + k_b).reshape(Bx, Tx, H, -1)
        att = jnp.einsum('bnhl,bmhl->bnmh', q, k)
        mask = src_mask.reshape(Bx, 1, Tx, 1)
        att = att + (1.0 - mask) * -1000000.0
        att = jax.nn.softmax(att, axis=2)
        v = ((xn @ v_w + v_b) * src_mask[:, :, None]).reshape(Bx, Tx, H, -1)
        y = jnp.einsum('bnmh,bmhl->bnhl', att, v).reshape(Bx, Tx, Dx)
        e = jax.nn.silu(emb) @ emb_w + emb_b
        scale, shift = jnp.split(e[:, None, :], 2, axis=2)
        h = layer_norm(y, sb_norm_w, sb_norm_b) * (1.0 + scale) + shift
        h = jax.nn.silu(h) @ out_w + out_b
        return x + h

    def _L1_cond_ref(x, c, ln_g, ln_b, ada_w, ada_b, in_proj_w, conv_w, conv_b, x_proj_w, dt_proj_w, dt_proj_b, A_log, D_param, out_proj_w):
        import jax, jax.numpy as jnp
        import numpy as np
        D = 512
        DI = 1024
        N = 16
        DT_RANK = 64
        D_CONV = 4
        EPS = 1e-05

        def _layernorm(x, g, b):
            mu = jnp.mean(x, axis=-1, keepdims=True)
            var = jnp.mean((x - mu) ** 2, axis=-1, keepdims=True)
            return (x - mu) * jax.lax.rsqrt(var + EPS) * g + b

        def _mamba(xn, in_proj_w, conv_w, conv_b, x_proj_w, dt_proj_w, dt_proj_b, A_log, D_param, out_proj_w):
            b, sl, _ = xn.shape
            xz = jnp.einsum('bsd,ed->bse', xn, in_proj_w)
            x_in, z = jnp.split(xz, 2, axis=-1)
            xt = jnp.transpose(x_in, (0, 2, 1))
            u = jax.lax.conv_general_dilated(xt, conv_w[:, None, :], (1,), [(D_CONV - 1, 0)], feature_group_count=DI, dimension_numbers=('NCH', 'OIH', 'NCH')) + conv_b[None, :, None]
            u = jax.nn.silu(jnp.transpose(u, (0, 2, 1)))
            x_dbl = jnp.einsum('bsd,ed->bse', u, x_proj_w)
            dt_r, B, C = jnp.split(x_dbl, [DT_RANK, DT_RANK + N], axis=-1)
            dt = jax.nn.softplus(jnp.einsum('bsr,dr->bsd', dt_r, dt_proj_w) + dt_proj_b)
            A = -jnp.exp(A_log)

            def step(h, inp):
                dt_t, B_t, C_t, u_t = inp
                dA = jnp.exp(dt_t[:, :, None] * A)
                h = h * dA + (dt_t * u_t)[:, :, None] * B_t[:, None, :]
                y = jnp.einsum('bdn,bn->bd', h, C_t)
                return (h, y)
            seq = (jnp.transpose(dt, (1, 0, 2)), jnp.transpose(B, (1, 0, 2)), jnp.transpose(C, (1, 0, 2)), jnp.transpose(u, (1, 0, 2)))
            h0 = jnp.zeros((b, DI, N), xn.dtype)
            _, ys = jax.lax.scan(step, h0, seq)
            y = jnp.transpose(ys, (1, 0, 2)) + u * D_param
            y = y * jax.nn.silu(z)
            return jnp.einsum('bsd,ed->bse', y, out_proj_w)
        ada = jnp.einsum('bc,ec->be', jax.nn.silu(c), ada_w) + ada_b
        shift, scale, gate = jnp.split(ada, 3, axis=1)
        xn = _layernorm(x, ln_g, ln_b)
        xn = xn * (1.0 + scale[:, None, :]) + shift[:, None, :]
        x_ssm = _mamba(xn, in_proj_w, conv_w, conv_b, x_proj_w, dt_proj_w, dt_proj_b, A_log, D_param, out_proj_w)
        return x + gate[:, None, :] * x_ssm
    x = _L0_cond_ref(x, cond_2048, mask_BxS_ff1, L0_cond_norm_w, L0_cond_norm_b, L0_cond_q_w, L0_cond_q_b, L0_cond_k_w, L0_cond_k_b, L0_cond_v_w, L0_cond_v_b, L0_cond_emb_w, L0_cond_emb_b, L0_cond_sb_norm_w, L0_cond_sb_norm_b, L0_cond_out_w, L0_cond_out_b)
    x = _L1_cond_ref(x, cond_2048, L1_cond_ln_g, L1_cond_ln_b, L1_cond_ada_w, L1_cond_ada_b, L1_cond_in_proj_w, L1_cond_conv_w, L1_cond_conv_b, L1_cond_x_proj_w, L1_cond_dt_proj_w, L1_cond_dt_proj_b, L1_cond_A_log, L1_cond_D_param, L1_cond_out_proj_w)
    return x

_drawn_inputs = setup_inputs


def setup_inputs(seed=0):
    import zlib

    import numpy as np

    out = dict(_drawn_inputs(seed))
    spreads = {'L0_cond_norm_w': (1.0, 0.2),
     'L0_cond_norm_b': (0.0, 0.1),
     'L0_cond_q_b': (0.0, 0.1),
     'L0_cond_k_b': (0.0, 0.1),
     'L0_cond_v_b': (0.0, 0.1),
     'L0_cond_emb_b': (0.0, 0.1),
     'L0_cond_sb_norm_w': (1.0, 0.2),
     'L0_cond_sb_norm_b': (0.0, 0.1),
     'L0_cond_out_b': (0.0, 0.1),
     'L1_cond_ln_g': (1.0, 0.2),
     'L1_cond_ln_b': (0.0, 0.1),
     'L1_cond_ada_b': (0.0, 0.1),
     'L1_cond_conv_b': (0.0, 0.1),
     'L1_cond_D_param': (1.0, 0.2)}
    factors = {}
    for name, (base, spread) in spreads.items():
        noise = np.random.default_rng([zlib.crc32(name.encode()), seed]).standard_normal(out[name].shape)
        drawn = base * np.exp(spread * noise) if base else spread * noise
        out[name] = jnp.asarray(drawn.astype(out[name].dtype))
    for name, factor in factors.items():
        out[name] = (out[name] * factor).astype(out[name].dtype)
    return out
```

```python
import numpy as np
from contextlib import ExitStack

import concourse.bass as bass
from concourse import mybir
from concourse.alu_op_type import AluOpType as ALU

F32 = mybir.dt.float32
ACT = mybir.ActivationFunctionType
P = 128
B, T, D = 8, 1024, 512
H, HD = 16, 32
TE = 1024
DI, NS, DTR, DC = 1024, 16, 64, 4
XD = DTR + 2 * NS
NT = T // P
KD = D // P
KE = TE // P
ND = DI // P
HG = P // HD
G = D // P
TB = T // 512
DG = 2
DL = ND // DG
EPS = 1e-5
BIG = 1e6
TILES = HG * NT
HALF = NT // 2
LAG = 6
PRO = 10

COLS = {}
_at = 0
for _name, _n in (("nw", KD), ("nb", KD), ("qb", KD), ("kb", KD), ("sw", KD), ("sb", KD), ("lg", KD), ("lb", KD),
                  ("cw", ND * DC), ("cb", ND), ("dtb", ND), ("alog", ND * NS), ("mask", B * NT)):
    COLS[_name] = (_at, _n)
    _at += _n
NPAR = _at


class Signal:

    def __init__(self, sem, per, first=0):
        self.sem, self.per, self.first = sem, per, first

    def reach(self, eng, b, n, alone=False):
        eng.wait_ge(self.sem, b * self.per + (n + self.first))
        if alone:
            eng.nop(nofuse=True)


def build(nc, x, condT, mask, params, q_w, k_w, v_w, v_b, emb_w, emb_b, out_w, out_b,
          adaT, ada_b, inT, xpT, dtT, D_row, opT, out):
    ctx = ExitStack()
    with ctx:
        def sb(name, shape):
            return ctx.enter_context(nc.sbuf_tensor(name, shape, F32))

        def sig(name, per, first=0):
            return Signal(ctx.enter_context(nc.semaphore(name)), per, first)

        b_rows = nc.dram_tensor("b_rows", (NS, T), F32).ap()
        gate_rows = nc.dram_tensor("gate_rows", (B, D), F32).ap()
        x1_keep = nc.dram_tensor("x1_keep", (P, NT * D), F32).ap()

        area_xT = sb("area_xT", [P, KD, T])
        area_w1 = sb("area_w1", [P, KD * T])
        area_w2 = sb("area_w2", [P, KD * T])
        area_u = sb("area_u", [P, ND * T])
        area_dt = sb("area_dt", [P, DL * T])
        area_h = sb("area_h", [P, 2 * DL * T])
        area_s = sb("area_s", [P, 4 * T])
        area_acc = sb("area_acc", [P, NT * DI])
        xdT = sb("xdT", [P, T])

        xT = area_xT
        X = area_u[:, 0:NT * D].rearrange("p (n d) -> p n d", n=NT)
        Y = area_u[:, NT * D:2 * NT * D].rearrange("p (n d) -> p n d", n=NT)
        xhat = area_dt[:, :].rearrange("p (n d) -> p n d", n=NT)
        q_pad = area_acc[:, 0:HG * T].rearrange("p (j t) -> p j t", j=HG)
        kT = area_acc[:, HG * T:(HG + 1) * T]
        V = area_acc[:, (HG + 1) * T:(HG + 2) * T].rearrange("p (m c) -> p m c", m=NT)
        mask_add = area_acc[:, (HG + 2) * T:(HG + 3) * T]
        yT = area_acc[:, (HG + 3) * T:(HG + 3) * T + 2 * P].rearrange("p (r c) -> p r c", r=2)
        PT = area_h[:, :].rearrange("p (r m c) -> p r m c", r=2, m=NT)
        S = area_s[:, 0:3 * T].rearrange("p (r t) -> p r t", r=3)
        wq = area_s[:, 3 * T:3 * T + KD * P].rearrange("p (k c) -> p k c", k=KD)
        wk = area_s[:, 3 * T + KD * P:4 * T].rearrange("p (k c) -> p k c", k=KD)
        wv = area_w1[:, 0:KD * D].rearrange("p (k c) -> p k c", k=KD)
        wo = area_w1[:, KD * D:2 * KD * D].rearrange("p (k c) -> p k c", k=KD)
        wx = area_w2[:, :].rearrange("p (k c) -> p k c", k=KD)
        wz = area_w1[:, :].rearrange("p (k c) -> p k c", k=KD)
        wp = area_w2[:, :].rearrange("p (k c) -> p k c", k=ND)
        U = area_u[:, :].rearrange("p (n t) -> p n t", n=ND)
        dT = area_dt[:, :].rearrange("p (n t) -> p n t", n=DL)
        hs = area_h[:, :].rearrange("p (r n t) -> p r n t", r=2, n=DL)
        dbu = area_s[:, 0:2 * T].rearrange("p (r t) -> p r t", r=2)
        bb = area_s[:, 2 * T:4 * T].rearrange("p (r t) -> p r t", r=2)
        acc = area_acc[:, :].rearrange("p (n d) -> p n d", n=NT)
        XW = T + 8
        xin = area_h[:, 0:2 * XW].rearrange("p (r t) -> p r t", r=2)
        cv = area_h[:, 2 * XW:2 * XW + 2 * T].rearrange("p (r t) -> p r t", r=2)
        dtmp = area_h[:, 0:2 * T].rearrange("p (r t) -> p r t", r=2)
        sz = area_h[:, 0:2 * DI].rearrange("p (r d) -> p r d", r=2)
        ygT = area_h[:, 2 * DI:4 * DI].rearrange("p (r k c) -> p r k c", r=2, k=ND)
        res = area_h[:, 4 * DI:4 * DI + 2 * D].rearrange("p (r d) -> p r d", r=2)
        x1t = area_h[:, 4 * DI + 2 * D:4 * DI + 4 * D].rearrange("p (r d) -> p r d", r=2)

        par = sb("par", [P, NPAR])

        def col(name, i, n=1):
            at = COLS[name][0]
            return par[:, at + i:at + i + n]

        ident = sb("ident", [P, P])
        vb_bc = sb("vb_bc", [P, D])
        ob_bc = sb("ob_bc", [P, D])
        gate_bc = sb("gate_bc", [P, D])
        D_bc = sb("D_bc", [P, DI])
        wxp = sb("wxp", [P, ND, XD])
        wdt = sb("wdt", [P, DI])
        C_nat = sb("C_nat", [P, NT, NS])
        negA = sb("negA", [P, ND * NS])
        gain0, shift0 = sb("gain0", [P, B * KD]), sb("shift0", [P, B * KD])
        gain1, shift1 = sb("gain1", [P, B * KD]), sb("shift1", [P, B * KD])
        stats = sb("stats", [P, NT, 6])
        mv = sb("mv", [P, NT, 2])
        rv = sb("rv", [P, NT])
        rstd = sb("rstd", [P, NT])
        nmr = sb("nmr", [P, NT])
        negmax = sb("negmax", [P, TILES])
        den = sb("den", [P, TILES])
        rden = sb("rden", [P, TILES])
        emb_st = area_h[:, :].rearrange("p (k c) -> p k c", k=KE)
        ada_st = [area_acc[:, k * 3 * D:(k + 1) * 3 * D] if k < 5 else area_u[:, (k - 5) * 3 * D:(k - 4) * 3 * D]
                  for k in range(KE)]
        silu_c = area_dt[:, 0:KE * B].rearrange("p (k b) -> p k b", k=KE)
        condc = area_dt[:, KE * B:2 * KE * B].rearrange("p (k b) -> p k b", k=KE)
        erow = area_xT[0:B, :, :].rearrange("p k t -> p (k t)")[:, 0:5 * D]
        ebias = area_s[0:B, 0:5 * D]
        one_plus = area_dt[:, 1024:1024 + KD * B].rearrange("p (k b) -> p k b", k=KD)
        prod = area_dt[:, 1536:1536 + KD * B].rearrange("p (k b) -> p k b", k=KD)
        ecol = area_dt[:, 2048:2048 + 4 * KD * B].rearrange("p (s k b) -> p s k b", s=4, k=KD)

        ps = ctx.enter_context(nc.psum_tensor("ps", [P, 8, 512], F32))

        def banks(i, n=TB):
            return ps[:, i:i + n, :].rearrange("p a c -> p (a c)")

        s_par = sig("params_loaded", 0)
        s_emb = sig("emb_loaded", 0)
        s_ones = sig("ident_ready", 0)
        s_silc = sig("silu_cond_ready", 0)
        s_ea = sig("exp_alog_ready", 0)
        s_er = sig("cond_rows_summed", 0)
        s_erb = sig("cond_rows_ready", 0)
        s_ec = sig("cond_cols_transposed", 0)
        s_pro = sig("prologue_vector", 0)
        s_gate = sig("gate_stored", 0)

        s_x = sig("x_loaded", 16)
        s_mask = sig("mask_loaded", 16)
        s_wvo = sig("wv_wo_loaded", 32)
        s_wqk = sig("wq_wk_loaded", 32 * G)
        s_wx = sig("wx_loaded", 16)
        s_wz = sig("wz_loaded", 16)
        s_wp = sig("wp_loaded", 16)
        s_gbc = sig("gate_broadcast", 16)
        s_x1s = sig("x1_stored", 16)
        s_x1l = [sig(f"x1_tile_loaded{r}", 16 * NT // 2) for r in range(2)]
        s_bst = sig("b_rows_stored", 16)
        s_bb = [sig(f"b_row_broadcast{r}", 16 * DG * NS // 2) for r in range(2)]
        s_out = [sig(f"out_stored{r}", 16 * NT // 2, 1) for r in range(2)]

        class Norm:

            def __init__(self, n):
                self.stats = sig(f"{n}_stats", NT)
                self.mv = sig(f"{n}_mean_var", NT)
                self.small = sig(f"{n}_small_steps", 3)
                self.rstd = sig(f"{n}_rstd", 1)
                self.xhat = sig(f"{n}_xhat", NT)
                self.tp = sig(f"{n}_transposed", 2 * KD)
                self.ready = sig(f"{n}_ready", 2 * KD)

        n0, n1, n2 = Norm("norm0"), Norm("norm1"), Norm("norm2")
        s_madd = sig("mask_bias_ready", 1)
        s_qz = sig("q_pad_zeroed", 1)
        s_xob = sig("x_plus_out_b", NT)
        s_qk = sig("qk_projected", 2 * G, 1)
        s_v = sig("v_projected", G)
        s_qev = sig("q_ready", G * HG)
        s_kev = sig("k_ready", G)
        s_vev = sig("v_ready", 2 * G)
        s_sc = sig("scores_ready", G * TILES)
        s_mx = sig("masked_and_max", G * TILES)
        s_ex = sig("exp_ready", G * TILES)
        s_pt = sig("probs_transposed", G * TILES * 2)
        s_pa = sig("probsT_copied_act", G * TILES)
        s_pv = sig("probsT_copied_dve", G * TILES)
        s_av = sig("av_ready", G * HG * 2)
        s_yc = sig("yT_copied", G * HG * 2)
        s_yt = sig("y_transposed", G * HG * 2)
        s_rd = sig("den_reciprocal", G * HG * 2)
        s_yn = sig("y_normalised", G * HG * 2)
        s_op = sig("attn_out_projected", NT)
        s_x1 = sig("x1_ready", NT)

        s_xz = sig("xin_pad_zeroed", 1)
        s_ip = sig("in_projected", ND)
        s_xe = sig("xin_copied", ND)
        s_c0 = sig("conv_last_tap", ND)
        s_cv = sig("conv_step", (DC - 1) * ND)
        s_u = sig("u_ready", ND)
        s_xd = sig("x_dbl_projected", 1)
        s_xde = sig("x_dbl_ready", 1)
        s_ct = sig("c_transposed", 1)
        s_cn = sig("c_ready", 1)
        s_ut = sig("u_transposed", NT)
        s_ai = sig("acc_started", NT)
        s_dp = sig("dt_projected", ND)
        s_dm = sig("dt_clamped", ND)
        s_de = sig("dt_exp", ND)
        s_dl = sig("dt_log", ND)
        s_dt = sig("dt_ready", ND)
        s_du = sig("dtu_ready", ND)
        UN = ND * NS
        s_dbu = sig("dbu_ready", UN, DL + 1)
        s_da = sig("da_ready", UN)
        s_h = sig("h_ready", UN, 2)
        s_ht = sig("h_transposed", DG * NS * NT, NT + 1)
        s_acc = sig("acc_added", DG * NS * NT, NT + 1)
        s_zp = sig("z_projected", NT, 1)
        s_sz = sig("silu_z_ready", NT)
        s_yg = sig("gated", NT, 1)
        s_ygt = sig("gated_transposed", NT)
        s_yge = sig("gatedT_ready", NT)
        s_o = sig("ssm_out_projected", NT, 1)
        s_og = sig("out_gated", NT, 1)
        s_oa = sig("out_ready", NT)

        block = ctx.enter_context(nc.Block())

        @block.sync
        def _(sp):
            for r in range(2):
                sp.sem_inc(s_out[r].sem, s_out[r].first)
            sp.dma_start(par[:, :], params).then_inc(s_par.sem, 16)
            sp.dma_start(condc, condT.rearrange("(k p) b -> p k b", p=P)).then_inc(s_par.sem, 16)
            sp.dma_start(ebias[:, 0:2 * D], emb_b.partition_broadcast(B)).then_inc(s_par.sem, 16)
            sp.dma_start(ebias[:, 2 * D:5 * D], ada_b.partition_broadcast(B)).then_inc(s_par.sem, 16)
            sp.dma_start(vb_bc[:, :], v_b.partition_broadcast(P)).then_inc(s_par.sem, 16)
            sp.dma_start(ob_bc[:, :], out_b.partition_broadcast(P)).then_inc(s_par.sem, 16)
            sp.dma_start(D_bc[:, :], D_row.partition_broadcast(P)).then_inc(s_par.sem, 16)
            sp.dma_start(wxp[:, :, :], xpT.rearrange("(k p) c -> p k c", p=P)).then_inc(s_par.sem, 16)
            sp.dma_start(wdt[0:DTR, :], dtT).then_inc(s_par.sem, 16)
            for k in range(KE):
                sp.dma_start(emb_st[:, k, :], emb_w[k * P:(k + 1) * P, :]).then_inc(s_emb.sem, 16)
                sp.dma_start(ada_st[k], adaT[k * P:(k + 1) * P, :]).then_inc(s_emb.sem, 16)
            sp.wait_ge(s_erb.sem, 1)
            sp.dma_start(gate_rows, erow[:, 4 * D:5 * D]).then_inc(s_gate.sem, 16)
            sp.wait_ge(s_gate.sem, 16)
            sp.wait_ge(s_pro.sem, PRO)
            with sp.Fori(0, B) as b:
                s_dbu.reach(sp, b, 0)
                sp.dma_start(X, x[bass.ds(b, 1), :, :].rearrange("a (n p) d -> p (a n) d", p=P)).then_inc(s_x.sem, 16)
                s_yg.reach(sp, b, 0)
                sp.dma_start(mask_add, mask[bass.ds(b, 1), :].rearrange("a t -> (a t)").partition_broadcast(P)
                             ).then_inc(s_mask.sem, 16)
                s_zp.reach(sp, b, 0)
                sp.dma_start(wv, v_w.rearrange("(k p) c -> p k c", p=P)).then_inc(s_wvo.sem, 16)
                sp.dma_start(wo, out_w.rearrange("(k p) c -> p k c", p=P)).then_inc(s_wvo.sem, 16)
                s_og.reach(sp, b, 0)
                sp.dma_start(gate_bc[:, :], gate_rows[bass.ds(b, 1), :].rearrange("a t -> (a t)").partition_broadcast(P)
                             ).then_inc(s_gbc.sem, 16)
                with sp.Fori(0, G) as g:
                    s_qk.reach(sp, b, g * 2)
                    sp.dma_start(wq, q_w[:, bass.ds(g * P, P)].rearrange("(k p) c -> p k c", p=P)).then_inc(s_wqk.sem, 16)
                    sp.dma_start(wk, k_w[:, bass.ds(g * P, P)].rearrange("(k p) c -> p k c", p=P)).then_inc(s_wqk.sem, 16)
                s_o.reach(sp, b, 0)
                sp.dma_start(wx, inT[:, 0:DI].rearrange("(k p) c -> p k c", p=P)).then_inc(s_wx.sem, 16)
                s_x1.reach(sp, b, NT)
                sp.dma_start(x1_keep, area_u[:, 0:NT * D]).then_inc(s_x1s.sem, 16)
                sp.dma_start(wz, inT[:, DI:2 * DI].rearrange("(k p) c -> p k c", p=P)).then_inc(s_wz.sem, 16)
                s_ip.reach(sp, b, ND)
                sp.dma_start(wp, opT.rearrange("(k p) c -> p k c", p=P)).then_inc(s_wp.sem, 16)
                s_xde.reach(sp, b, 1)
                sp.dma_start(b_rows, xdT[DTR:DTR + NS, :]).then_inc(s_bst.sem, 16)
                s_bst.reach(sp, b, 16, alone=True)
                for dg in range(DG):
                    with sp.Fori(0, NS // 2) as i:
                        for q in range(2):
                            s_dbu.reach(sp, b, i * (2 * DL) + DL * (dg * NS + q - 1))
                            sp.dma_start(bb[:, q, :], b_rows[bass.ds(i * 2 + q, 1), :].rearrange("a t -> (a t)")
                                         .partition_broadcast(P)).then_inc(s_bb[q].sem, 16)
                s_acc.reach(sp, b, DG * NS * NT)
                s_x1s.reach(sp, b, 16)
                for n in range(2):
                    sp.dma_start(x1t[:, n, :], x1_keep[:, n * D:(n + 1) * D]).then_inc(s_x1l[n].sem, 16)
                for n in range(NT):
                    s_oa.reach(sp, b, n + 1)
                    sp.dma_start(out[bass.ds(b, 1), n * P:(n + 1) * P, :].rearrange("a p d -> (a p) d"),
                                 res[:, n % 2, :]).then_inc(s_out[n % 2].sem, 16)
                    if n + 2 < NT:
                        sp.dma_start(x1t[:, n % 2, :], x1_keep[:, (n + 2) * D:(n + 3) * D]).then_inc(s_x1l[n % 2].sem, 16)
            for r in range(2):
                sp.wait_ge(s_out[r].sem, s_out[r].first + B * NT // 2 * 16)

        @block.gpsimd
        def _(pool):
            pool.sem_inc(s_dbu.sem, s_dbu.first)
            pool.memset(ident[:, :], 0.0).then_inc(s_ones.sem, 1)
            pool.wait_ge(s_ones.sem, 1)
            pool.memset(wdt[DTR:P, :], 0.0).then_inc(s_ones.sem, 1)
            pool.wait_ge(s_ones.sem, 2)
            pool.memset(xdT[XD:P, :], 0.0).then_inc(s_ones.sem, 1)
            pool.wait_ge(s_ones.sem, 3)
            pool.affine_select(out=ident[:, :], in_=ident[:, :], compare_op=ALU.not_equal, fill=1.0, base=0,
                               pattern=[[-1, P]], channel_multiplier=1).then_inc(s_ones.sem, 1)
            pool.wait_ge(s_pro.sem, PRO)
            with pool.Fori(0, B) as b:
                s_yg.reach(pool, b, 0, alone=True)
                pool.memset(area_acc[:, 0:HG * T], 0.0).then_inc(s_qz.sem, 1)
                for n in range(NT):
                    n0.xhat.reach(pool, b, NT)
                    pool.tensor_tensor(X[:, n, :], X[:, n, :], ob_bc[:, :], ALU.add).then_inc(s_xob.sem, 1)
                for dg in range(DG):
                    for dl in range(DL):
                        n = dg * DL + dl
                        s_dt.reach(pool, b, n + 1)
                        if n == 0:
                            s_ut.reach(pool, b, NT)
                        pool.tensor_tensor(U[:, n, :], U[:, n, :], dT[:, dl, :], ALU.mult).then_inc(s_du.sem, 1)
                    with pool.Fori(0, NS // 2) as i:
                        for q in range(2):
                            for dl in range(DL):
                                k = (dg * NS + q) * DL + dl
                                if q == 0:
                                    s_du.reach(pool, b, dg * DL + dl + 1)
                                if dl == 0:
                                    s_bb[q].reach(pool, b, i * 16 + 16 * (dg * NS // 2 + 1))
                                s_h.reach(pool, b, i * (2 * DL) + k - 1)
                                pool.tensor_tensor(dbu[:, dl % 2, :], U[:, dg * DL + dl, :], bb[:, q, :], ALU.mult
                                                   ).then_inc(s_dbu.sem, 1)

        @block.scalar
        def _(act):
            act.wait_ge(s_par.sem, 16 * 9)
            nc.scalar.activation(silu_c, condc, ACT.Silu).then_inc(s_silc.sem, 1)
            nc.scalar.activation(negA[:, :], col("alog", 0, ND * NS), ACT.Exp).then_inc(s_ea.sem, 1)

            def norm_act(N, b, gains, shifts, func):
                N.small.reach(act, b, 2)
                nc.scalar.activation(rstd[:, :], rv[:, :], ACT.Sqrt).then_inc(N.rstd.sem, 1)
                for hf in range(2):
                    for k in range(KD):
                        N.tp.reach(act, b, hf * KD + k + 1, alone=True)
                        nc.scalar.activation(xT[:, k, hf * 512:(hf + 1) * 512], ps[:, hf * KD + k, :], func,
                                             scale=gains(k), bias=shifts(k)).then_inc(N.ready.sem, 1)

            act.wait_ge(s_pro.sem, PRO)
            with act.Fori(0, B) as b:
                norm_act(n0, b, lambda k: col("nw", k), lambda k: col("nb", k), ACT.Identity)
                with act.Fori(0, G) as g:
                    s_qk.reach(act, b, g * 2 + 1)
                    s_qz.reach(act, b, 1, alone=True)
                    for j in range(HG):
                        rows = slice(j * HD, (j + 1) * HD)
                        nc.scalar.activation(q_pad[rows, j, :], banks(0)[rows, :], ACT.Identity,
                                             bias=par[rows, bass.ds(g + COLS["qb"][0], 1)]).then_inc(s_qev.sem, 1)
                    for s in range(TILES + 2):
                        if s < TILES:
                            s_mx.reach(act, b, g * TILES + s + 1)
                            nc.scalar.activation(S[:, s % 3, :], S[:, s % 3, :], ACT.Exp, scale=-1.0,
                                                 bias=negmax[:, s:s + 1], accum_out=den[:, s:s + 1]).then_inc(s_ex.sem, 1)
                        t = s - 2
                        if t >= 0:
                            s_pt.reach(act, b, g * (2 * TILES) + 2 * t + 2)
                            if t % HALF == 0:
                                half = t // HALF
                                if half >= 2:
                                    s_av.reach(act, b, g * (2 * HG) + half - 1)
                                elif half == 0:
                                    for r in range(2):
                                        s_out[r].reach(act, b, 0)
                            c = t % HALF
                            nc.scalar.activation(PT[:, (t // HALF) % 2, HALF:NT, c * P:(c + 1) * P],
                                                 ps[:, 4 + (2 * t + 1) % 3, :].rearrange("p (m c) -> p m c", m=HALF),
                                                 ACT.Copy).then_inc(s_pa.sem, 1)
                norm_act(n1, b, lambda k: gain0[:, bass.ds(b * KD + k, 1)], lambda k: shift0[:, bass.ds(b * KD + k, 1)],
                         ACT.Silu)
                norm_act(n2, b, lambda k: gain1[:, bass.ds(b * KD + k, 1)], lambda k: shift1[:, bass.ds(b * KD + k, 1)],
                         ACT.Identity)
                s_xz.reach(act, b, 1)
                for n in range(ND + 1):
                    if n < ND:
                        s_ip.reach(act, b, n + 1)
                        if n >= 2:
                            s_cv.reach(act, b, (DC - 1) * (n - 1))
                        nc.scalar.activation(xin[:, n % 2, DC - 1:DC - 1 + T], banks(2 * (n % 4)), ACT.Copy
                                             ).then_inc(s_xe.sem, 1)
                        if n >= 2:
                            s_u.reach(act, b, n - 1)
                        nc.scalar.activation(cv[:, n % 2, :], banks(2 * (n % 4)), ACT.Identity,
                                             scale=col("cw", n * DC + DC - 1), bias=col("cb", n)).then_inc(s_c0.sem, 1)
                    m = n - 1
                    if m >= 0:
                        if m == 0:
                            s_x1s.reach(act, b, 16)
                        s_cv.reach(act, b, (DC - 1) * (m + 1))
                        nc.scalar.activation(U[:, m, :], cv[:, m % 2, :], ACT.Silu).then_inc(s_u.sem, 1)
                s_xd.reach(act, b, 1)
                nc.scalar.activation(xdT[0:XD, :], banks(0)[0:XD, :], ACT.Copy).then_inc(s_xde.sem, 1)
                for dg in range(DG):
                    for dl in range(DL):
                        n = dg * DL + dl
                        s_dm.reach(act, b, n + 1)
                        nc.scalar.activation(dtmp[:, dl % 2, :], dtmp[:, dl % 2, :], ACT.Exp).then_inc(s_de.sem, 1)
                        s_de.reach(act, b, n + 1)
                        nc.scalar.activation(dtmp[:, dl % 2, :], dtmp[:, dl % 2, :], ACT.Ln, bias=1.0).then_inc(s_dl.sem, 1)
                    s_dt.reach(act, b, (dg + 1) * DL, alone=True)
                    with act.Fori(0, NS // 2) as i:
                        for q in range(2):
                            for dl in range(DL):
                                k = (dg * NS + q) * DL + dl
                                s_h.reach(act, b, i * (2 * DL) + k - 1, alone=True)
                                nc.scalar.activation(banks(2 * (dl % 2)), dT[:, dl, :], ACT.Exp,
                                                     scale=negA[:, bass.ds(i * 2 + ((dg * DL + dl) * NS + q), 1)]
                                                     ).then_inc(s_da.sem, 1)
                for s in range(NT + 1):
                    if s < NT:
                        s_zp.reach(act, b, s + 1)
                        if s >= 2:
                            s_yg.reach(act, b, s - 1)
                        elif s == 0:
                            s_acc.reach(act, b, DG * NS * NT)
                        nc.scalar.activation(sz[:, s % 2, :], banks(2 * (s % 2)), ACT.Silu).then_inc(s_sz.sem, 1)
                    t = s - 1
                    if t >= 0:
                        s_ygt.reach(act, b, t + 1)
                        if t >= 2:
                            s_o.reach(act, b, t - 1)
                        nc.scalar.activation(ygT[:, t % 2, :, :].rearrange("p k c -> p (k c)"), banks(4), ACT.Copy
                                             ).then_inc(s_yge.sem, 1)

        @block.vector
        def _(dve):
            v = nc.vector
            dve.sem_inc(s_h.sem, s_h.first)
            dve.sem_inc(s_acc.sem, s_acc.first)
            dve.sem_inc(s_yg.sem, s_yg.first)
            dve.sem_inc(s_og.sem, s_og.first)
            dve.wait_ge(s_er.sem, 1)
            v.tensor_tensor(erow, ps[0:B, 0:5, :].rearrange("p a c -> p (a c)"), ebias, ALU.add).then_inc(s_erb.sem, 1)
            dve.wait_ge(s_ec.sem, 1)
            v.tensor_copy(ecol.rearrange("p s k b -> p (s k b)"), ps[:, 5, 0:4 * KD * B]).then_inc(s_pro.sem, 1)
            dve.wait_ge(s_pro.sem, 1)
            at = 1
            for scale_i, shift_i, w, bb_, gain, shift in ((0, 1, "sw", "sb", gain0, shift0), (3, 2, "lg", "lb", gain1, shift1)):
                def by_b(a):
                    return a[:, :].rearrange("p (b k) -> p k b", k=KD)

                def chan(name):
                    return col(name, 0, KD).unsqueeze(2).to_broadcast([P, KD, B])

                v.tensor_scalar_add(one_plus, ecol[:, scale_i], 1.0).then_inc(s_pro.sem, 1)
                dve.wait_ge(s_pro.sem, at + 1)
                v.tensor_tensor(by_b(gain), one_plus, chan(w), ALU.mult).then_inc(s_pro.sem, 1)
                v.tensor_tensor(prod, one_plus, chan(bb_), ALU.mult).then_inc(s_pro.sem, 1)
                dve.wait_ge(s_pro.sem, at + 3)
                v.tensor_tensor(by_b(shift), prod, ecol[:, shift_i], ALU.add).then_inc(s_pro.sem, 1)
                dve.wait_ge(s_pro.sem, at + 4)
                at += 4
            dve.wait_ge(s_ea.sem, 1)
            v.tensor_scalar_mul(negA[:, :], negA[:, :], -1.0).then_inc(s_pro.sem, 1)
            assert at + 1 == PRO
            dve.wait_ge(s_pro.sem, PRO)

            def norm_dve(N, b, src, arrived):
                for n in range(NT):
                    arrived(n)
                    v.bn_stats(stats[:, n, :], src[:, n, :]).then_inc(N.stats.sem, 1)
                for n in range(NT):
                    N.stats.reach(dve, b, n + 1, alone=True)
                    v.bn_aggr(mv[:, n, :], stats[:, n, :]).then_inc(N.mv.sem, 1)
                N.mv.reach(dve, b, NT)
                v.tensor_scalar_add(rv[:, :], mv[:, :, 1], EPS).then_inc(N.small.sem, 1)
                N.small.reach(dve, b, 1)
                v.reciprocal(rv[:, :], rv[:, :]).then_inc(N.small.sem, 1)
                N.rstd.reach(dve, b, 1)
                v.scalar_tensor_tensor(out=nmr[:, :], in0=mv[:, :, 0], scalar=-1.0, in1=rstd[:, :],
                                       op0=ALU.mult, op1=ALU.mult).then_inc(N.small.sem, 1)
                N.small.reach(dve, b, 3)
                for n in range(NT):
                    v.tensor_scalar(xhat[:, n, :], src[:, n, :], rstd[:, n:n + 1], nmr[:, n:n + 1],
                                    ALU.mult, ALU.add).then_inc(N.xhat.sem, 1)

            with dve.Fori(0, B) as b:
                norm_dve(n0, b, X, lambda n: s_x.reach(dve, b, 16) if n == 0 else None)
                s_mask.reach(dve, b, 16)
                v.tensor_scalar(mask_add, mask_add, -1.0, BIG, ALU.add, ALU.mult).then_inc(s_madd.sem, 1)
                s_madd.reach(dve, b, 1)
                s_wvo.reach(dve, b, 32, alone=True)
                with dve.Fori(0, G) as g:
                    s_qk.reach(dve, b, g * 2 + 2)
                    v.tensor_scalar(kT, banks(2), par[:, bass.ds(g + COLS["kb"][0], 1)], None, ALU.add
                                    ).then_inc(s_kev.sem, 1)
                    s_v.reach(dve, b, g + 1)
                    v.tensor_tensor(V, banks(4).rearrange("p (m c) -> p m c", m=NT),
                                    vb_bc[:, bass.ds(g * P, P)].unsqueeze(1).to_broadcast([P, NT, P]), ALU.add
                                    ).then_inc(s_vev.sem, 1)
                    s_vev.reach(dve, b, g * 2 + 1)
                    v.tensor_tensor(V, V, par[:, bass.ds(b * NT + COLS["mask"][0], NT)].unsqueeze(2)
                                    .to_broadcast([P, NT, P]), ALU.mult).then_inc(s_vev.sem, 1)
                    for s in range(TILES + LAG):
                        if s < TILES:
                            s_sc.reach(dve, b, g * TILES + s + 1)
                            if s >= 3:
                                s_pt.reach(dve, b, g * (2 * TILES) + 2 * (s - 2))
                            dve.nop(nofuse=True)
                            v.tensor_tensor_reduce(out=S[:, s % 3, :], in0=banks(2 * (s % 2)), in1=mask_add,
                                                   scale=-1.0, scalar=3.0e38, op0=ALU.add, op1=ALU.min,
                                                   accum_out=negmax[:, s:s + 1]).then_inc(s_mx.sem, 1)
                        t = s - 2
                        if 0 <= t < TILES:
                            s_pt.reach(dve, b, g * (2 * TILES) + 2 * t + 1)
                            if t % HALF == 0:
                                half = t // HALF
                                if half >= 2:
                                    s_av.reach(dve, b, g * (2 * HG) + half - 1)
                                elif half == 0:
                                    for r in range(2):
                                        s_out[r].reach(dve, b, 0)
                            c = t % HALF
                            v.tensor_copy(PT[:, (t // HALF) % 2, 0:HALF, c * P:(c + 1) * P],
                                          ps[:, 4 + (2 * t) % 3, :].rearrange("p (m c) -> p m c", m=HALF)
                                          ).then_inc(s_pv.sem, 1)
                        t = s - 4
                        if 0 <= t < TILES and t % HALF == HALF - 1:
                            half = t // HALF
                            s_av.reach(dve, b, g * (2 * HG) + half + 1)
                            if half >= 2:
                                s_yt.reach(dve, b, g * (2 * HG) + half - 1)
                            v.tensor_copy(yT[:, half % 2, :], ps[:, 7, (half % 2) * P:(half % 2 + 1) * P]
                                          ).then_inc(s_yc.sem, 1)
                            s_ex.reach(dve, b, g * TILES + t + 1)
                            v.reciprocal(rden[:, t - 3:t + 1], den[:, t - 3:t + 1]).then_inc(s_rd.sem, 1)
                        t = s - 6
                        if t >= 0 and t % HALF == HALF - 1:
                            half = t // HALF
                            j, hf = half // 2, half % 2
                            s_yt.reach(dve, b, g * (2 * HG) + half + 1)
                            s_rd.reach(dve, b, g * (2 * HG) + half + 1)
                            v.tensor_tensor(Y[:, hf * HALF:(hf + 1) * HALF, bass.ds(g * P + j * HD, HD)],
                                            ps[:, 7, 2 * P + (half % 2) * P:2 * P + (half % 2 + 1) * P]
                                            .rearrange("p (c l) -> p c l", l=HD),
                                            rden[:, t - 3:t + 1].unsqueeze(2).to_broadcast([P, HALF, HD]), ALU.mult
                                            ).then_inc(s_yn.sem, 1)
                s_yn.reach(dve, b, G * HG * 2)
                norm_dve(n1, b, Y, lambda n: None)
                for n in range(NT):
                    s_op.reach(dve, b, n + 1)
                    s_xob.reach(dve, b, n + 1)
                    v.tensor_tensor(X[:, n, :], ps[:, n, :], X[:, n, :], ALU.add).then_inc(s_x1.sem, 1)
                norm_dve(n2, b, X, lambda n: s_x1.reach(dve, b, n + 1))
                v.memset(xin[:, :, 0:DC - 1], 0.0).then_inc(s_xz.sem, 1)
                for n in range(ND):
                    s_c0.reach(dve, b, n + 1)
                    for i in range(DC - 1):
                        if i:
                            s_cv.reach(dve, b, (DC - 1) * n + i)
                        v.scalar_tensor_tensor(out=cv[:, n % 2, :], in0=xin[:, n % 2, i:i + T],
                                               scalar=col("cw", n * DC + i), in1=cv[:, n % 2, :],
                                               op0=ALU.mult, op1=ALU.add).then_inc(s_cv.sem, 1)
                s_ct.reach(dve, b, 1)
                v.tensor_copy(C_nat[:, :, :], banks(2).rearrange("p (n c) -> p n c", n=NT)[:, :, DTR + NS:XD]
                              ).then_inc(s_cn.sem, 1)
                for n in range(NT):
                    s_ut.reach(dve, b, n + 1)
                    v.tensor_tensor(acc[:, n, :], banks(4 + 2 * (n % 2)), D_bc[:, :], ALU.mult).then_inc(s_ai.sem, 1)
                s_ai.reach(dve, b, NT)
                s_cn.reach(dve, b, 1)
                for dg in range(DG):
                    if dg:
                        s_ht.reach(dve, b, dg * NS * NT)
                    for dl in range(DL + 1):
                        if dl < DL:
                            n = dg * DL + dl
                            s_dp.reach(dve, b, n + 1)
                            if dl >= 2:
                                s_dt.reach(dve, b, n - 1)
                            v.tensor_scalar(dtmp[:, dl % 2, :], banks(2 * (dl % 2)), col("dtb", n), 30.0,
                                            ALU.add, ALU.min).then_inc(s_dm.sem, 1)
                        m = dl - 1
                        if m >= 0:
                            n = dg * DL + m
                            s_dl.reach(dve, b, n + 1)
                            v.scalar_tensor_tensor(out=dT[:, m, :], in0=banks(2 * (m % 2)), scalar=col("dtb", n),
                                                   in1=dtmp[:, m % 2, :], op0=ALU.add, op1=ALU.max
                                                   ).then_inc(s_dt.sem, 1)
                    s_dt.reach(dve, b, (dg + 1) * DL, alone=True)
                    with dve.Fori(0, NS // 2) as i:
                        def scan(q, dl):
                            k = (dg * NS + q) * DL + dl
                            s_da.reach(dve, b, i * (2 * DL) + k + 1)
                            s_dbu.reach(dve, b, i * (2 * DL) + k + 1)
                            if dl == 0:
                                s_ht.reach(dve, b, i * (2 * NT) + NT * (dg * NS + q - 1))
                            v.tensor_tensor_scan(out=hs[:, q, dl, :], data0=banks(2 * (dl % 2)), data1=dbu[:, dl % 2, :],
                                                 initial=0.0, op0=ALU.mult, op1=ALU.add).then_inc(s_h.sem, 1)

                        def add(q, n):
                            k = (dg * NS + q) * NT + n
                            s_ht.reach(dve, b, i * (2 * NT) + k + 1)
                            s_acc.reach(dve, b, i * (2 * NT) + k + 1 - NT)
                            part = acc[:, n, dg * 512:(dg + 1) * 512]
                            v.scalar_tensor_tensor(out=part, in0=ps[:, 4 + n % 4, :],
                                                   scalar=C_nat[:, n, bass.ds(i * 2 + q, 1)], in1=part,
                                                   op0=ALU.mult, op1=ALU.add).then_inc(s_acc.sem, 1)

                        for dl in range(DL):
                            scan(0, dl)
                        for dl in range(DL):
                            scan(1, dl)
                            add(0, 2 * dl)
                            add(0, 2 * dl + 1)
                        for n in range(NT):
                            add(1, n)
                s_acc.reach(dve, b, DG * NS * NT)
                s_gbc.reach(dve, b, 16)
                for s in range(NT + 2):
                    if s < NT:
                        s_sz.reach(dve, b, s + 1)
                        v.tensor_tensor(acc[:, s, :], acc[:, s, :], sz[:, s % 2, :], ALU.mult).then_inc(s_yg.sem, 1)
                    t = s - 2
                    if t >= 0:
                        s_o.reach(dve, b, t + 1)
                        if t >= 2:
                            s_out[t % 2].reach(dve, b, 16 * (t // 2))
                        v.tensor_tensor(res[:, t % 2, :], ps[:, 6 + t % 2, :], gate_bc[:, :], ALU.mult
                                        ).then_inc(s_og.sem, 1)
                        s_og.reach(dve, b, t + 1)
                        s_x1l[t % 2].reach(dve, b, 16 * (t // 2 + 1))
                        v.tensor_tensor(res[:, t % 2, :], res[:, t % 2, :], x1t[:, t % 2, :], ALU.add
                                        ).then_inc(s_oa.sem, 1)

        @block.tensor
        def _(pe):
            pe.sem_inc(s_qk.sem, s_qk.first)
            pe.sem_inc(s_ht.sem, s_ht.first)
            pe.sem_inc(s_zp.sem, s_zp.first)
            pe.sem_inc(s_o.sem, s_o.first)

            def mm(out, lhsT, rhs, k, last):
                return nc.tensor.matmul(out, lhsT, rhs, start=(k == 0), stop=(k == last))

            pe.wait_ge(s_silc.sem, 1)
            pe.wait_ge(s_emb.sem, 16 * 2 * KE)
            for k in range(KE):
                for c in range(2):
                    mm(ps[0:B, c, :], silu_c[:, k, :], emb_st[:, k, c * 512:(c + 1) * 512], k, KE - 1)
                for c in range(3):
                    last = mm(ps[0:B, 2 + c, :], silu_c[:, k, :], ada_st[k][:, c * 512:(c + 1) * 512], k, KE - 1)
            last.then_inc(s_er.sem, 1)
            pe.wait_ge(s_erb.sem, 1)
            pe.wait_ge(s_ones.sem, 4)
            for c in range(4 * KD):
                last = nc.tensor.transpose(ps[:, 5, c * B:(c + 1) * B], erow[:, c * P:(c + 1) * P], ident[0:B, 0:B])
            last.then_inc(s_ec.sem, 1)

            def norm_pe(N, b):
                for hf in range(2):
                    N.xhat.reach(pe, b, (hf + 1) * HALF)
                    for k in range(KD):
                        for c in range(HALF):
                            last = nc.tensor.transpose(ps[:, hf * KD + k, c * P:(c + 1) * P],
                                                       xhat[:, hf * HALF + c, k * P:(k + 1) * P], ident[:, :])
                        last.then_inc(N.tp.sem, 1)

            with pe.Fori(0, B) as b:
                s_og.reach(pe, b, 0)
                norm_pe(n0, b)
                n0.ready.reach(pe, b, 2 * KD)
                s_wvo.reach(pe, b, 32, alone=True)
                with pe.Fori(0, G) as g:
                    s_wqk.reach(pe, b, g * 32 + 32)
                    for w, bank in ((wq, 0), (wk, 2)):
                        for th in range(TB):
                            for k in range(KD):
                                last = mm(ps[:, bank + th, :], w[:, k, :], xT[:, k, th * 512:(th + 1) * 512], k, KD - 1)
                        last.then_inc(s_qk.sem, 1)
                    for n in range(NT):
                        for k in range(KD):
                            last = mm(ps[:, 4 + n // 4, (n % 4) * P:(n % 4 + 1) * P], xT[:, k, n * P:(n + 1) * P],
                                      wv[:, k, bass.ds(g * P, P)], k, KD - 1)
                    last.then_inc(s_v.sem, 1)
                    s_kev.reach(pe, b, g + 1)
                    for s in range(TILES + LAG):
                        if s < TILES:
                            j, n = s // NT, s % NT
                            if n == 0:
                                s_qev.reach(pe, b, g * HG + (HG if s == 0 else j + 1))
                            if s >= 2:
                                s_mx.reach(pe, b, g * TILES + s - 1)
                            for th in range(TB):
                                last = mm(ps[:, 2 * (s % 2) + th, :], q_pad[:, j, n * P:(n + 1) * P],
                                          kT[:, th * 512:(th + 1) * 512], 0, 0)
                            last.then_inc(s_sc.sem, 1)
                        t = s - 2
                        if 0 <= t < TILES:
                            s_ex.reach(pe, b, g * TILES + t + 1)
                            if t == 0:
                                s_vev.reach(pe, b, g * 2 + 2)
                            for c in range(2):
                                unit = 2 * t + c
                                if unit >= 3:
                                    if unit % 2:
                                        s_pv.reach(pe, b, g * TILES + (unit - 3) // 2 + 1)
                                    else:
                                        s_pa.reach(pe, b, g * TILES + (unit - 3) // 2 + 1)
                                for m in range(HALF):
                                    last = nc.tensor.transpose(ps[:, 4 + unit % 3, m * P:(m + 1) * P],
                                                               S[:, t % 3, (c * HALF + m) * P:(c * HALF + m + 1) * P],
                                                               ident[:, :])
                                last.then_inc(s_pt.sem, 1)
                        t = s - 4
                        if 0 <= t < TILES and t % HALF == HALF - 1:
                            half = t // HALF
                            s_pv.reach(pe, b, g * TILES + t + 1)
                            s_pa.reach(pe, b, g * TILES + t + 1)
                            if half:
                                s_yn.reach(pe, b, g * (2 * HG) + half)
                            j = half // 2
                            for m in range(NT):
                                for c in range(HG):
                                    last = mm(ps[c * HD:(c + 1) * HD, 7, (half % 2) * P:(half % 2 + 1) * P],
                                              V[:, m, j * HD:(j + 1) * HD], PT[:, half % 2, m, c * P:(c + 1) * P],
                                              m, NT - 1)
                            last.then_inc(s_av.sem, 1)
                        t = s - 6
                        if t >= 0 and t % HALF == HALF - 1:
                            half = t // HALF
                            s_yc.reach(pe, b, g * (2 * HG) + half + 1)
                            nc.tensor.transpose(ps[:, 7, 2 * P + (half % 2) * P:2 * P + (half % 2 + 1) * P],
                                                yT[:, half % 2, :], ident[:, :]).then_inc(s_yt.sem, 1)
                s_yn.reach(pe, b, G * HG * 2)
                norm_pe(n1, b)
                for n in range(NT):
                    n1.ready.reach(pe, b, KD * (n // HALF + 1))
                    for k in range(KD):
                        last = mm(ps[:, n, :], xT[:, k, n * P:(n + 1) * P], wo[:, k, :], k, KD - 1)
                    last.then_inc(s_op.sem, 1)
                norm_pe(n2, b)
                n2.ready.reach(pe, b, 2 * KD)
                s_wx.reach(pe, b, 16)
                for n in range(ND):
                    if n >= 4:
                        s_c0.reach(pe, b, n - 3)
                    for th in range(TB):
                        for k in range(KD):
                            last = mm(ps[:, 2 * (n % 4) + th, :], wx[:, k, n * P:(n + 1) * P],
                                      xT[:, k, th * 512:(th + 1) * 512], k, KD - 1)
                    last.then_inc(s_ip.sem, 1)
                for n in range(ND):
                    s_u.reach(pe, b, n + 1)
                    if n == 0:
                        s_c0.reach(pe, b, 5)
                    for th in range(TB):
                        last = mm(ps[0:XD, th, :], wxp[:, n, :], U[:, n, th * 512:(th + 1) * 512], n, ND - 1)
                last.then_inc(s_xd.sem, 1)
                for n in range(NT):
                    if n >= 2:
                        s_ai.reach(pe, b, n - 1)
                    for k in range(ND):
                        last = nc.tensor.transpose(ps[:, 4 + 2 * (n % 2) + k // 4, (k % 4) * P:(k % 4 + 1) * P],
                                                   U[:, k, n * P:(n + 1) * P], ident[:, :])
                    last.then_inc(s_ut.sem, 1)
                    if n == 1:
                        s_xde.reach(pe, b, 1)
                        for m in range(NT):
                            last = nc.tensor.transpose(ps[:, 2 + m // 4, (m % 4) * P:(m % 4 + 1) * P],
                                                       xdT[:, m * P:(m + 1) * P], ident[:, :])
                        last.then_inc(s_ct.sem, 1)
                s_cn.reach(pe, b, 1)
                s_ai.reach(pe, b, NT)
                for dg in range(DG):
                    if dg:
                        s_h.reach(pe, b, dg * NS * DL)
                    for dl in range(DL):
                        n = dg * DL + dl
                        if dl >= 2:
                            s_dt.reach(pe, b, n - 1)
                        for th in range(TB):
                            last = mm(ps[:, 2 * (dl % 2) + th, :], wdt[:, n * P:(n + 1) * P],
                                      xdT[:, th * 512:(th + 1) * 512], 0, 0)
                        last.then_inc(s_dp.sem, 1)
                    with pe.Fori(0, NS // 2) as i:
                        for q in range(2):
                            s_h.reach(pe, b, i * (2 * DL) + (dg * NS + q + 1) * DL)
                            for n in range(NT):
                                s_acc.reach(pe, b, i * (2 * NT) + (dg * NS + q) * NT + n - 3)
                                for dl in range(DL):
                                    last = nc.tensor.transpose(ps[:, 4 + n % 4, dl * P:(dl + 1) * P],
                                                               hs[:, q, dl, n * P:(n + 1) * P], ident[:, :])
                                last.then_inc(s_ht.sem, 1)
                s_acc.reach(pe, b, DG * NS * NT)
                s_wz.reach(pe, b, 16)
                for s in range(NT + 2):
                    if s < NT:
                        if s >= 2:
                            s_sz.reach(pe, b, s - 1)
                        for c in range(2):
                            for k in range(KD):
                                last = mm(ps[:, 2 * (s % 2) + c, :], xT[:, k, s * P:(s + 1) * P],
                                          wz[:, k, c * 512:(c + 1) * 512], k, KD - 1)
                        last.then_inc(s_zp.sem, 1)
                    t = s - 1
                    if 0 <= t < NT:
                        s_yg.reach(pe, b, t + 1)
                        if t >= 1:
                            s_yge.reach(pe, b, t)
                        for k in range(ND):
                            last = nc.tensor.transpose(ps[:, 4 + k // 4, (k % 4) * P:(k % 4 + 1) * P],
                                                       acc[:, t, k * P:(k + 1) * P], ident[:, :])
                        last.then_inc(s_ygt.sem, 1)
                    t = s - 2
                    if t >= 0:
                        s_yge.reach(pe, b, t + 1)
                        if t == 0:
                            s_wp.reach(pe, b, 16)
                        if t >= 2:
                            s_og.reach(pe, b, t - 1)
                        for k in range(ND):
                            last = mm(ps[:, 6 + t % 2, :], ygT[:, t % 2, k, :], wp[:, k, :], k, ND - 1)
                        last.then_inc(s_o.sem, 1)
    return nc


def kernel(**inputs):
    import concourse.bacc as bacc
    from concourse.bass_utils import run_bass_kernel_spmd

    def get(name):
        return np.asarray(inputs[name])

    def cols(a):
        return a.reshape(-1, P).T

    l0, l1 = "L0_cond_", "L1_cond_"
    A_log = get(l1 + "A_log").reshape(ND, P, NS).transpose(1, 0, 2).reshape(P, ND * NS)
    conv_w = get(l1 + "conv_w").reshape(ND, P, DC).transpose(1, 0, 2).reshape(P, ND * DC)
    mask = get("mask_BxS_ff1")
    packed = {
        "nw": cols(get(l0 + "norm_w")), "nb": cols(get(l0 + "norm_b")), "qb": cols(get(l0 + "q_b")),
        "kb": cols(get(l0 + "k_b")), "sw": cols(get(l0 + "sb_norm_w")), "sb": cols(get(l0 + "sb_norm_b")),
        "lg": cols(get(l1 + "ln_g")), "lb": cols(get(l1 + "ln_b")), "cw": conv_w, "cb": cols(get(l1 + "conv_b")),
        "dtb": cols(get(l1 + "dt_proj_b")), "alog": A_log, "mask": cols(mask.reshape(-1)),
    }
    arrays = {
        "x": get("x"), "condT": get("cond_2048").T, "mask": mask,
        "params": np.concatenate([packed[name] for name in COLS], axis=1),
        "q_w": get(l0 + "q_w"), "k_w": get(l0 + "k_w"), "v_w": get(l0 + "v_w"), "v_b": get(l0 + "v_b"),
        "emb_w": get(l0 + "emb_w"), "emb_b": get(l0 + "emb_b"), "out_w": get(l0 + "out_w"), "out_b": get(l0 + "out_b"),
        "adaT": get(l1 + "ada_w").T, "ada_b": get(l1 + "ada_b"), "inT": get(l1 + "in_proj_w").T,
        "xpT": get(l1 + "x_proj_w").T, "dtT": get(l1 + "dt_proj_w").T, "D_row": get(l1 + "D_param"),
        "opT": get(l1 + "out_proj_w").T,
    }
    arrays = {name: np.ascontiguousarray(a) for name, a in arrays.items()}
    nc = bacc.Bacc("TRN2", target_bir_lowering=False, num_devices=1)
    args = [nc.dram_tensor(name, a.shape, mybir.dt.from_np(a.dtype), kind="ExternalInput").ap()
            for name, a in arrays.items()]
    args.append(nc.dram_tensor("out", (B, T, D), F32, kind="ExternalOutput").ap())
    build(nc, *args)
    r = run_bass_kernel_spmd(nc, [arrays], core_ids=[0])
    return r.results[0]["out"]
```

```python
import numpy as np
from contextlib import ExitStack

import concourse.bass as bass
from concourse import mybir
from concourse.alu_op_type import AluOpType as ALU

F32 = mybir.dt.float32
F32R = mybir.dt.float32r
ACT = mybir.ActivationFunctionType
P = 128
B, T, D = 8, 1024, 512
H, HD = 16, 32
TE = 1024
DI, NS, DTR, DC = 1024, 16, 64, 4
XD = DTR + 2 * NS
NT = T // P
KD = D // P
KE = TE // P
ND = DI // P
HG = P // HD
G = D // P
TB = T // 512
DG = 2
ZU = NT * 2
DL = ND // DG
EPS = 1e-5
BIG = 1e6
TILES = HG * NT
HALF = NT // 2
SR = 4
M_LAG, T_LAG, A_LAG = 1, 3, 4
C_LAG = A_LAG + HALF - 1
Y_LAG = C_LAG + 1
AV_KEYS = ((0, 1, 2), (3, 4, 5), (6, 7), ())
CHUNKS, CHUNK_AT, CHUNK_STEPS, CHUNK_K = 2 * TB, 2 * NT + 1, 4, (0, 0, 1, 2)


def chunk_out(s):
    c, step = divmod(s - CHUNK_AT, CHUNK_STEPS)
    return c if 0 <= c < CHUNKS and step == CHUNK_STEPS - 1 else None


def columns(i, n):
    return slice(i, i + n) if isinstance(i, int) else bass.ds(i, n)

PRO = 10

COLS = {}
_at = 0
for _name, _n in (("nw", KD), ("nb", KD), ("qb", KD), ("kb", KD), ("sw", KD), ("sb", KD), ("lg", KD), ("lb", KD),
                  ("cw", ND * DC), ("cb", ND), ("dtb", ND), ("alog", ND * NS), ("mask", B * NT)):
    COLS[_name] = (_at, _n)
    _at += _n
NPAR = _at


class Signal:

    def __init__(self, sem, per, first=0):
        self.sem, self.per, self.first = sem, per, first

    def at(self, b, n):
        return self.sem, b * self.per + (n + self.first)


def build(nc, x, condT, mask, params, q_w, k_w, v_w, v_b, emb_w, emb_b, out_w, out_b,
          adaT, ada_b, inT, xpT, dtT, D_row, opT, out):
    ctx = ExitStack()
    with ctx:
        def sb(name, shape):
            return ctx.enter_context(nc.sbuf_tensor(name, shape, F32))

        def sig(name, per, first=0):
            return Signal(ctx.enter_context(nc.semaphore(name)), per, first)

        b_rows = nc.dram_tensor("b_rows", (NS, T), F32).ap()
        gate_rows = nc.dram_tensor("gate_rows", (B, D), F32).ap()
        x1_keep = nc.dram_tensor("x1_keep", (P, NT * D), F32).ap()
        z_keep = nc.dram_tensor("z_keep", (P, NT * DI), F32).ap()

        area_xT = sb("area_xT", [P, KD, T])
        area_w1 = sb("area_w1", [P, KD * T])
        area_w2 = sb("area_w2", [P, KD * T])
        area_u = sb("area_u", [P, ND * T])
        area_dt = sb("area_dt", [P, DL * T])
        area_h = sb("area_h", [P, 2 * DL * T])
        area_s = sb("area_s", [P, 4 * T])
        area_acc = sb("area_acc", [P, NT * DI])
        xdT = sb("xdT", [P, T])

        xT = area_xT
        X = area_u[:, 0:NT * D].rearrange("p (n d) -> p n d", n=NT)
        Y = area_u[:, NT * D:2 * NT * D].rearrange("p (n d) -> p n d", n=NT)
        xhat = area_dt[:, :].rearrange("p (n d) -> p n d", n=NT)
        q_part = [area_acc[:, i * T:(i + 1) * T] for i in range(2)]
        k_part = [area_acc[:, (2 + i) * T:(3 + i) * T] for i in range(2)]
        V = area_acc[:, 4 * T:5 * T].rearrange("p (m c) -> p m c", m=NT)
        mask_add = area_acc[:, 5 * T:6 * T]
        yT = area_acc[:, 6 * T:6 * T + 2 * P].rearrange("p (r c) -> p r c", r=2)
        q_stack = ctx.enter_context(nc.sbuf_tensor("q_stack", [P, 2, T], F32R))
        k_stack = ctx.enter_context(nc.sbuf_tensor("k_stack", [P, 2, T], F32R))
        PT = area_h[:, :].rearrange("p (r m c) -> p r m c", r=2, m=NT)
        S = area_s[:, 0:SR * T].rearrange("p (r t) -> p r t", r=SR)
        wq = area_w2[:, 2 * D:2 * D + KD * P].rearrange("p (k c) -> p k c", k=KD)
        wk = area_w2[:, 2 * D + KD * P:2 * D + 2 * KD * P].rearrange("p (k c) -> p k c", k=KD)
        wv = area_w1[:, 0:KD * D].rearrange("p (k c) -> p k c", k=KD)
        wo = area_w1[:, KD * D:2 * KD * D].rearrange("p (k c) -> p k c", k=KD)
        wx = area_w2[:, :].rearrange("p (k c) -> p k c", k=KD)
        wz = area_w1[:, :].rearrange("p (k c) -> p k c", k=KD)
        wp = area_w2[:, :].rearrange("p (k c) -> p k c", k=ND)
        U = area_u[:, :].rearrange("p (n t) -> p n t", n=ND)
        dT = area_dt[:, :].rearrange("p (n t) -> p n t", n=DL)
        hs = area_h[:, :].rearrange("p (r n t) -> p r n t", r=2, n=DL)
        dbu = area_s[:, 0:2 * T].rearrange("p (r t) -> p r t", r=2)
        bb = area_s[:, 2 * T:4 * T].rearrange("p (r t) -> p r t", r=2)
        acc = area_acc[:, :].rearrange("p (n d) -> p n d", n=NT)
        XW = T + 8
        xin = area_h[:, 0:2 * XW].rearrange("p (r t) -> p r t", r=2)
        cv = area_h[:, 2 * XW:2 * XW + 2 * T].rearrange("p (r t) -> p r t", r=2)
        dtmp = area_h[:, 0:DL * T].rearrange("p (r t) -> p r t", r=DL)
        wxp = area_h[:, 5 * T:5 * T + ND * XD].rearrange("p (k c) -> p k c", k=ND)
        D_bc = area_h[:, 6 * T:7 * T]
        sz = area_s[:, 2 * T:2 * T + 2 * DI].rearrange("p (r d) -> p r d", r=2)
        ygT = area_h[:, 2 * DI:4 * DI].rearrange("p (r k c) -> p r k c", r=2, k=ND)
        res = area_h[:, 4 * DI:4 * DI + 2 * D].rearrange("p (r d) -> p r d", r=2)
        x1t = area_h[:, 4 * DI + 2 * D:4 * DI + 4 * D].rearrange("p (r d) -> p r d", r=2)

        gate_bc = area_h[:, 4 * DI + 4 * D:4 * DI + 5 * D]

        par = sb("par", [P, NPAR])

        def col(name, i, n=1):
            at = COLS[name][0]
            return par[:, at + i:at + i + n]

        ident = sb("ident", [P, P])
        vb_bc = area_w2[:, 0:D]
        ob_bc = area_w2[:, D:2 * D]
        wdt = sb("wdt", [P, DI])
        C_nat = sb("C_nat", [P, NT, NS])
        negA = sb("negA", [P, ND * NS])
        gain0, shift0 = sb("gain0", [P, B * KD]), sb("shift0", [P, B * KD])
        gain1, shift1 = sb("gain1", [P, B * KD]), sb("shift1", [P, B * KD])
        stats = sb("stats", [P, NT, 6])
        mv = sb("mv", [P, NT, 2])
        rv = sb("rv", [P, NT])
        rstd = sb("rstd", [P, NT])
        nmr = sb("nmr", [P, NT])
        negmax = sb("negmax", [P, TILES])
        den = sb("den", [P, TILES])
        rden = sb("rden", [P, TILES])
        warm = sb("warm", [P, 1])
        z_st = sb("z_st", [P, 512])
        emb_st = area_h[:, :].rearrange("p (k c) -> p k c", k=KE)
        ada_st = [area_acc[:, k * 3 * D:(k + 1) * 3 * D] if k < 5 else area_u[:, (k - 5) * 3 * D:(k - 4) * 3 * D]
                  for k in range(KE)]
        silu_c = area_dt[:, 0:KE * B].rearrange("p (k b) -> p k b", k=KE)
        condc = area_dt[:, KE * B:2 * KE * B].rearrange("p (k b) -> p k b", k=KE)
        erow = area_xT[0:B, :, :].rearrange("p k t -> p (k t)")[:, 0:5 * D]
        ebias = area_s[0:B, 0:5 * D]
        one_plus = area_dt[:, 1024:1024 + KD * B].rearrange("p (k b) -> p k b", k=KD)
        prod = area_dt[:, 1536:1536 + KD * B].rearrange("p (k b) -> p k b", k=KD)
        ecol = area_dt[:, 2048:2048 + 4 * KD * B].rearrange("p (s k b) -> p s k b", s=4, k=KD)

        ps = ctx.enter_context(nc.psum_tensor("ps", [P, 8, 512], F32))

        def banks(i, n=TB):
            return ps[:, i:i + n, :].rearrange("p a c -> p (a c)")

        s_par = sig("params_loaded", 0)
        s_emb = sig("emb_loaded", 0)
        s_ones = sig("ident_ready", 0)
        s_silc = sig("silu_cond_ready", 0)
        s_ea = sig("exp_alog_ready", 0)
        s_warm = sig("exp_table_loaded", 0)
        s_er = sig("cond_rows_summed", 0)
        s_erb = sig("cond_rows_ready", 0)
        s_ec = sig("cond_cols_transposed", 0)
        s_pro = sig("prologue_vector", 0)
        s_gate = sig("gate_stored", 0)

        s_x = sig("x_loaded", 16)
        s_mask = sig("mask_loaded", 16)
        s_wvo = sig("wv_wo_biases_loaded", 64)
        s_stk = [sig(f"qk_stacked{r}", 128 * G * HG // 2, 1) for r in range(2)]
        s_xpd = sig("wxp_D_loaded", 32)
        s_wqk = sig("wq_wk_loaded", 32 * G)
        s_wx = sig("wx_loaded", 16)
        s_wz = sig("wz_loaded", 16)
        s_wp = sig("wp_loaded", 16)
        s_gbc = sig("gate_broadcast", 16)
        s_x1s = sig("x1_stored", 16)
        s_x1l = [sig(f"x1_tile_loaded{r}", 16 * NT // 2) for r in range(2)]
        s_bst = sig("b_rows_stored", 16)
        s_bb = [sig(f"b_row_broadcast{r}", 16 * DG * NS // 2) for r in range(2)]
        s_out = [sig(f"out_stored{r}", 16 * NT // 2, 1) for r in range(2)]

        class Norm:

            def __init__(self, n):
                self.stats = sig(f"{n}_stats", NT)
                self.mv = sig(f"{n}_mean_var", NT)
                self.eps = sig(f"{n}_var_eps", 2)
                self.inv = sig(f"{n}_inverse_var", 2)
                self.rstd = sig(f"{n}_rstd", 2)
                self.shift = sig(f"{n}_mean_rstd", 2)
                self.xhat = sig(f"{n}_xhat", NT)
                self.tp = sig(f"{n}_transposed", 2 * KD)
                self.ready = sig(f"{n}_ready", 2 * KD)

        n0, n1, n2 = Norm("norm0"), Norm("norm1"), Norm("norm2")
        s_madd = sig("mask_bias_ready", 1)
        s_xob = sig("x_plus_out_b", NT)
        s_qk = sig("qk_projected", CHUNKS * G, 1)
        s_v = sig("v_projected", G)
        s_hi = sig("qk_hi_ready", CHUNKS * G)
        s_lo = sig("qk_lo_ready", CHUNKS * G)
        s_vev = sig("v_ready", 2 * G)
        s_sc = sig("scores_ready", G * TILES, NT + 1)
        s_mx = sig("masked_and_max", G * TILES)
        s_ex = sig("exp_ready", G * TILES)
        s_pt = sig("probs_transposed", G * TILES * 2)
        s_pa = sig("probsT_copied_act", G * TILES)
        s_pv = sig("probsT_copied_dve", G * TILES)
        s_av = sig("av_ready", G * HG * 2)
        s_yc = sig("yT_copied", G * HG * 2)
        s_yt = sig("y_transposed", G * HG * 2)
        s_rd = sig("den_reciprocal", G * HG * 2)
        s_yn = sig("y_normalised", G * HG * 2)
        s_op = sig("attn_out_projected", NT)
        s_x1 = sig("x1_ready", NT)

        s_xz = sig("xin_pad_zeroed", 1)
        s_ip = sig("in_projected", ND)
        s_xe = sig("xin_copied", ND)
        s_c0 = sig("conv_last_tap", ND)
        s_cv = sig("conv_step", (DC - 1) * ND)
        s_u = sig("u_ready", ND)
        s_xd = sig("x_dbl_projected", 1)
        s_xde = sig("x_dbl_ready", 1)
        s_ct = sig("c_transposed", 1)
        s_cn = sig("c_ready", 1)
        s_ut = sig("u_transposed", NT)
        s_ai = sig("acc_started", NT)
        s_dp = sig("dt_projected", ND)
        s_dm = sig("dt_clamped", ND)
        s_de = sig("dt_exp", ND)
        s_dl = sig("dt_log", ND)
        s_dt = sig("dt_ready", ND)
        s_du = sig("dtu_ready", ND)
        UN = ND * NS
        s_dbu = sig("dbu_ready", UN, DL + 1)
        s_da = sig("da_ready", UN)
        s_h = sig("h_ready", UN, 2)
        s_ht = sig("h_transposed", DG * NS * NT, NT + 1)
        s_acc = sig("acc_added", DG * NS * NT, NT + 1)
        s_zp = sig("z_projected", ZU, 1)
        s_zc = sig("z_copied", ZU)
        s_zs = sig("z_stored", 16 * ZU, 1)
        s_zl = [sig(f"z_tile_loaded{r}", 16 * NT // 2) for r in range(2)]
        s_sz = sig("silu_z_ready", NT)
        s_yg = sig("gated", NT, 1)
        s_ygt = sig("gated_transposed", NT)
        s_yge = sig("gatedT_ready", NT)
        s_o = sig("ssm_out_projected", NT, 1)
        s_og = sig("out_gated", NT, 1)
        s_oa = sig("out_ready", NT)

        block = ctx.enter_context(nc.Block())

        @block.sync
        def _(sp):
            for r in range(2):
                sp.sem_inc(s_out[r].sem, s_out[r].first)
                sp.sem_inc(s_stk[r].sem, s_stk[r].first)
            sp.sem_inc(s_zs.sem, s_zs.first)
            sp.dma_start(par[:, :], params).then_inc(s_par.sem, 16)
            sp.dma_start(condc, condT.rearrange("(k p) b -> p k b", p=P)).then_inc(s_par.sem, 16)
            sp.dma_start(ebias[:, 0:2 * D], emb_b.partition_broadcast(B)).then_inc(s_par.sem, 16)
            sp.dma_start(ebias[:, 2 * D:5 * D], ada_b.partition_broadcast(B)).then_inc(s_par.sem, 16)
            sp.dma_start(wdt[0:DTR, :], dtT).then_inc(s_par.sem, 16)
            for k in range(KE):
                sp.dma_start(emb_st[:, k, :], emb_w[k * P:(k + 1) * P, :]).then_inc(s_emb.sem, 16)
                sp.dma_start(ada_st[k], adaT[k * P:(k + 1) * P, :]).then_inc(s_emb.sem, 16)
            sp.wait_ge(s_erb.sem, 1)
            sp.dma_start(gate_rows, erow[:, 4 * D:5 * D]).then_inc(s_gate.sem, 16)
            sp.wait_ge(s_gate.sem, 16)
            sp.wait_ge(s_pro.sem, PRO)
            with sp.Fori(0, B) as b:
                sp.wait_ge(*s_o.at(b, 0))
                sp.nop(nofuse=True)

                def load_wqk(g):
                    sp.dma_start(wq, q_w[:, columns(g * P, P)].rearrange("(k p) c -> p k c", p=P)).then_inc(s_wqk.sem, 16)
                    sp.dma_start(wk, k_w[:, columns(g * P, P)].rearrange("(k p) c -> p k c", p=P)).then_inc(s_wqk.sem, 16)

                def stack_heads(g, last):
                    for j in range(HG):
                        sp.wait_ge(*s_sc.at(b, g * TILES + (j - 1) * NT))
                        for parts, stack, order, done in ((q_part, q_stack, (0, 0, 1, 1), TB),
                                                          (k_part, k_stack, (0, 1, 0, 1), 2 * TB)):
                            if j == 0:
                                sp.wait_ge(*s_hi.at(b, g * CHUNKS + done))
                                sp.wait_ge(*s_lo.at(b, g * CHUNKS + done))
                            for c, part in enumerate(order):
                                sp.dma_start(stack[c * HD:(c + 1) * HD, j % 2, :].bitcast(F32),
                                             parts[part][j * HD:(j + 1) * HD, :]
                                             ).then_inc(s_stk[j % 2].sem, 16)
                        if j == 1 and not last:
                            sp.wait_ge(*s_qk.at(b, g * CHUNKS + CHUNKS))
                            load_wqk(g + 1)

                load_wqk(0)
                with sp.Fori(0, G - 1) as g:
                    stack_heads(g, False)
                stack_heads(G - 1, True)
                sp.wait_ge(*s_xob.at(b, NT))
                sp.wait_ge(*s_vev.at(b, 2 * G))
                sp.dma_start(wx, inT[:, 0:DI].rearrange("(k p) c -> p k c", p=P)).then_inc(s_wx.sem, 16)
                sp.wait_ge(*s_av.at(b, G * HG * 2))
                sp.dma_start(wxp, xpT.rearrange("(k p) c -> p k c", p=P)).then_inc(s_xpd.sem, 16)
                sp.dma_start(D_bc, D_row.partition_broadcast(P)).then_inc(s_xpd.sem, 16)
                sp.wait_ge(*s_x1.at(b, NT))
                sp.dma_start(x1_keep, area_u[:, 0:NT * D]).then_inc(s_x1s.sem, 16)
                sp.dma_start(wz, inT[:, DI:2 * DI].rearrange("(k p) c -> p k c", p=P)).then_inc(s_wz.sem, 16)
                sp.wait_ge(*s_ip.at(b, ND))
                sp.dma_start(wp, opT.rearrange("(k p) c -> p k c", p=P)).then_inc(s_wp.sem, 16)
                sp.wait_ge(*s_xde.at(b, 1))
                sp.dma_start(b_rows, xdT[DTR:DTR + NS, :]).then_inc(s_bst.sem, 16)
                sp.wait_ge(*s_bst.at(b, 16))
                sp.nop(nofuse=True)
                for dg in range(DG):
                    with sp.Fori(0, NS // 2) as i:
                        for q in range(2):
                            sp.wait_ge(*s_dbu.at(b, i * (2 * DL) + DL * (dg * NS + q - 1)))
                            sp.dma_start(bb[:, q, :], b_rows[bass.ds(i * 2 + q, 1), :].rearrange("a t -> (a t)")
                                         .partition_broadcast(P)).then_inc(s_bb[q].sem, 16)
                def load_z(n):
                    sp.dma_start(sz[:, n % 2, :], z_keep[:, n * DI:(n + 1) * DI]).then_inc(s_zl[n % 2].sem, 16)

                def load_x1(n):
                    sp.dma_start(x1t[:, n % 2, :], x1_keep[:, n * D:(n + 1) * D]).then_inc(s_x1l[n % 2].sem, 16)

                sp.wait_ge(*s_zs.at(b, 16 * 4))
                sp.nop(nofuse=True)
                for n in range(2):
                    sp.wait_ge(*s_dbu.at(b, UN - DL * (1 - n)))
                    sp.nop(nofuse=True)
                    load_z(n)
                sp.wait_ge(*s_acc.at(b, DG * NS * NT))
                sp.nop(nofuse=True)
                sp.wait_ge(*s_x1s.at(b, 16))
                sp.nop(nofuse=True)
                sp.wait_ge(*s_zs.at(b, 16 * ZU))
                sp.nop(nofuse=True)

                load_x1(0)
                load_x1(1)
                sp.dma_start(gate_bc, gate_rows[bass.ds(b, 1), :].rearrange("a t -> (a t)").partition_broadcast(P)
                             ).then_inc(s_gbc.sem, 16)
                sp.wait_ge(*s_yg.at(b, 1))
                load_z(2)
                for n in range(NT):
                    if n + 3 < NT:
                        sp.wait_ge(*s_yg.at(b, n + 2))
                        load_z(n + 3)
                    sp.wait_ge(*s_oa.at(b, n + 1))
                    sp.dma_start(out[bass.ds(b, 1), n * P:(n + 1) * P, :].rearrange("a p d -> (a p) d"),
                                 res[:, n % 2, :]).then_inc(s_out[n % 2].sem, 16)
                    if n + 2 < NT:
                        load_x1(n + 2)
            for r in range(2):
                sp.wait_ge(s_out[r].sem, s_out[r].first + B * NT // 2 * 16)

        @block.gpsimd
        def _(pool):
            pool.sem_inc(s_dbu.sem, s_dbu.first)
            pool.memset(ident[:, :], 0.0).then_inc(s_ones.sem, 1)
            pool.wait_ge(s_ones.sem, 1)
            pool.memset(wdt[DTR:P, :], 0.0).then_inc(s_ones.sem, 1)
            pool.wait_ge(s_ones.sem, 2)
            pool.memset(xdT[XD:P, :], 0.0).then_inc(s_ones.sem, 1)
            pool.wait_ge(s_ones.sem, 3)
            pool.affine_select(out=ident[:, :], in_=ident[:, :], compare_op=ALU.not_equal, fill=1.0, base=0,
                               pattern=[[-1, P]], channel_multiplier=1).then_inc(s_ones.sem, 1)
            pool.wait_ge(s_pro.sem, PRO)
            pool.dma_start(X, x[0:1, :, :].rearrange("a (n p) d -> p (a n) d", p=P)).then_inc(s_x.sem, 16)
            with pool.Fori(0, B) as b:
                pool.wait_ge(*s_yg.at(b, 0))
                pool.nop(nofuse=True)
                pool.dma_start(mask_add, mask[bass.ds(b, 1), :].rearrange("a t -> (a t)").partition_broadcast(P)
                             ).then_inc(s_mask.sem, 16)
                pool.wait_ge(*s_zp.at(b, 0))
                pool.nop(nofuse=True)
                pool.dma_start(wv, v_w.rearrange("(k p) c -> p k c", p=P)).then_inc(s_wvo.sem, 16)
                pool.dma_start(wo, out_w.rearrange("(k p) c -> p k c", p=P)).then_inc(s_wvo.sem, 16)
                pool.wait_ge(*s_o.at(b, 0))
                pool.nop(nofuse=True)
                pool.dma_start(vb_bc, v_b.partition_broadcast(P)).then_inc(s_wvo.sem, 16)
                pool.dma_start(ob_bc, out_b.partition_broadcast(P)).then_inc(s_wvo.sem, 16)
                pool.wait_ge(*s_wvo.at(b, 64))
                for n in range(NT):
                    pool.wait_ge(*n0.xhat.at(b, NT))
                    pool.tensor_tensor(X[:, n, :], X[:, n, :], ob_bc[:, :], ALU.add).then_inc(s_xob.sem, 1)
                for dg in range(DG):
                    with pool.Fori(0, NS // 2) as i:
                        for q in range(2):
                            for dl in range(DL):
                                k = (dg * NS + q) * DL + dl
                                if q == 0:
                                    pool.wait_ge(*s_du.at(b, dg * DL + dl + 1))
                                if dl == 0:
                                    pool.wait_ge(*s_bb[q].at(b, i * 16 + 16 * (dg * NS // 2 + 1)))
                                pool.wait_ge(*s_h.at(b, i * (2 * DL) + k - 1))
                                pool.tensor_tensor(dbu[:, dl % 2, :], U[:, dg * DL + dl, :], bb[:, q, :], ALU.mult
                                                   ).then_inc(s_dbu.sem, 1)
                pool.wait_ge(*s_dbu.at(b, UN))
                pool.nop(nofuse=True)
                pool.dma_start(X, x[bass.ds((b + 1) & (B - 1), 1), :, :].rearrange("a (n p) d -> p (a n) d", p=P)
                               ).then_inc(s_x.sem, 16)

        @block.scalar
        def _(act):
            act.wait_ge(s_par.sem, 16 * 5)
            nc.scalar.activation(silu_c, condc, ACT.Silu).then_inc(s_silc.sem, 1)
            nc.scalar.activation(negA[:, :], col("alog", 0, ND * NS), ACT.Exp).then_inc(s_ea.sem, 1)

            def root(N, b):
                for hf in range(2):
                    rows = slice(hf * HALF, (hf + 1) * HALF)
                    act.wait_ge(*N.inv.at(b, hf + 1))
                    nc.scalar.activation(rstd[:, rows], rv[:, rows], ACT.Sqrt).then_inc(N.rstd.sem, 1)

            def affine(N, b, gains, shifts, func):
                for hf in range(2):
                    for k in range(KD):
                        act.wait_ge(*N.tp.at(b, hf * KD + k + 1))
                        act.nop(nofuse=True)
                        nc.scalar.activation(xT[:, k, hf * 512:(hf + 1) * 512], ps[:, hf * KD + k, :], func,
                                             scale=gains(k), bias=shifts(k)).then_inc(N.ready.sem, 1)

            act.wait_ge(s_gate.sem, 16)
            act.wait_ge(s_pro.sem, PRO)
            root(n0, 0)
            with act.Fori(0, B) as b:
                affine(n0, b, lambda k: col("nw", k), lambda k: col("nb", k), ACT.Identity)
                nc.scalar.activation(warm[:, :], negA[:, 0:1], ACT.Exp).then_inc(s_warm.sem, 1)

                def high_part(g, c, bank):
                    part, name = ((q_part, "qb"), (k_part, "kb"))[c // TB]
                    act.wait_ge(*s_qk.at(b, g * CHUNKS + c + 1))
                    act.nop(nofuse=True)
                    if c == 0:
                        for r in range(2):
                            act.wait_ge(*s_stk[r].at(b, g * 256))
                            act.nop(nofuse=True)
                    nc.scalar.activation(part[0][:, (c % TB) * 512:(c % TB + 1) * 512].bitcast(F32R), ps[:, bank, :],
                                         ACT.Identity, bias=par[:, columns(g + COLS[name][0], 1)]).then_inc(s_hi.sem, 1)

                def attend_act(g, last):
                    for s in range(M_LAG, TILES + T_LAG):
                        if not last and chunk_out(s) is not None:
                            high_part(g + 1, chunk_out(s), 7)
                        t = s - M_LAG
                        if t < TILES:
                            act.wait_ge(*s_mx.at(b, g * TILES + t + 1))
                            nc.scalar.activation(S[:, t % SR, :], S[:, t % SR, :], ACT.Exp, scale=-1.0,
                                                 bias=negmax[:, t:t + 1], accum_out=den[:, t:t + 1]).then_inc(s_ex.sem, 1)
                        t = s - T_LAG
                        if t >= 0:
                            act.wait_ge(*s_pt.at(b, g * (2 * TILES) + 2 * t + 2))
                            if t % HALF == 0:
                                half = t // HALF
                                if half >= 2:
                                    act.wait_ge(*s_av.at(b, g * (2 * HG) + half - 1))
                                elif half == 0:
                                    for r in range(2):
                                        act.wait_ge(*s_out[r].at(b, 0))
                            c = t % HALF
                            nc.scalar.activation(PT[:, (t // HALF) % 2, HALF:NT, c * P:(c + 1) * P],
                                                 ps[:, 5, :].rearrange("p (m c) -> p m c", m=HALF),
                                                 ACT.Copy).then_inc(s_pa.sem, 1)

                for c in range(CHUNKS):
                    high_part(0, c, c)
                with act.Fori(0, G - 1) as g:
                    attend_act(g, False)
                attend_act(G - 1, True)
                root(n1, b)
                affine(n1, b, lambda k: gain0[:, bass.ds(b * KD + k, 1)], lambda k: shift0[:, bass.ds(b * KD + k, 1)],
                       ACT.Silu)
                root(n2, b)
                affine(n2, b, lambda k: gain1[:, bass.ds(b * KD + k, 1)], lambda k: shift1[:, bass.ds(b * KD + k, 1)],
                         ACT.Identity)
                act.wait_ge(*s_xz.at(b, 1))
                for n in range(ND + 1):
                    if n < ND:
                        act.wait_ge(*s_ip.at(b, n + 1))
                        if n >= 2:
                            act.wait_ge(*s_cv.at(b, (DC - 1) * (n - 1)))
                        nc.scalar.activation(xin[:, n % 2, DC - 1:DC - 1 + T], banks(2 * (n % 4)), ACT.Copy
                                             ).then_inc(s_xe.sem, 1)
                        if n >= 2:
                            act.wait_ge(*s_u.at(b, n - 1))
                        nc.scalar.activation(cv[:, n % 2, :], banks(2 * (n % 4)), ACT.Identity,
                                             scale=col("cw", n * DC + DC - 1), bias=col("cb", n)).then_inc(s_c0.sem, 1)
                    m = n - 1
                    if m >= 0:
                        if m == 0:
                            act.wait_ge(*s_x1s.at(b, 16))
                        act.wait_ge(*s_cv.at(b, (DC - 1) * (m + 1)))
                        nc.scalar.activation(U[:, m, :], cv[:, m % 2, :], ACT.Silu).then_inc(s_u.sem, 1)
                act.wait_ge(*s_xd.at(b, 1))
                nc.scalar.activation(xdT[0:XD, :], banks(0)[0:XD, :], ACT.Copy).then_inc(s_xde.sem, 1)
                for dg in range(DG):

                    def decay(r, z_unit, tiles=range(DL)):
                        for dl in tiles:
                            k = (dg * NS + r) * DL + dl
                            if isinstance(r, int) and r == 0:
                                act.wait_ge(*s_dt.at(b, dg * DL + dl + 1))
                                act.nop(nofuse=True)
                            act.wait_ge(*s_h.at(b, k - 1))
                            act.nop(nofuse=True)
                            a_col = r + (dg * DL + dl) * NS
                            a_col = negA[:, a_col:a_col + 1] if isinstance(r, int) else negA[:, bass.ds(a_col, 1)]
                            nc.scalar.activation(banks(2 * (dl % 2)), dT[:, dl, :], ACT.Exp, scale=a_col
                                                 ).then_inc(s_da.sem, 1)
                            if dl == 0 and z_unit is not None:
                                keep_z(z_unit)

                    def keep_z(u):
                        k = u + dg * NS // 2
                        act.wait_ge(*s_zp.at(b, k + 1))
                        act.nop(nofuse=True)
                        act.wait_ge(*s_zs.at(b, k * 16))
                        act.nop(nofuse=True)
                        nc.scalar.activation(z_st[:, :], ps[:, 7, :], ACT.Copy).then_inc(s_zc.sem, 1)
                        act.wait_ge(*s_zc.at(b, k + 1))
                        act.nop(nofuse=True)
                        cols = slice(k * 512, (k + 1) * 512) if isinstance(k, int) else bass.ds(k * 512, 512)
                        act.dma_start(z_keep[:, cols], z_st[:, :]).then_inc(s_zs.sem, 16)

                    for pair in (0, 2):
                        for dl in (pair, pair + 1):
                            act.wait_ge(*s_dm.at(b, dg * DL + dl + 1))
                            nc.scalar.activation(dtmp[:, dl, :], dtmp[:, dl, :], ACT.Exp).then_inc(s_de.sem, 1)
                        if pair:
                            decay(0, None, (0, 1))
                        for dl in (pair, pair + 1):
                            act.wait_ge(*s_de.at(b, dg * DL + dl + 1))
                            nc.scalar.activation(dtmp[:, dl, :], dtmp[:, dl, :], ACT.Ln, bias=1.0).then_inc(s_dl.sem, 1)
                    decay(0, None, (2, 3))
                    decay(1, None)
                    with act.Fori(0, NS // 2 - 1) as i:
                        decay(i * 2 + 2, None)
                        decay(i * 2 + 3, i)
                    keep_z(NS // 2 - 1)
                for s in range(NT + 1):
                    if s < NT:
                        act.wait_ge(*s_zl[s % 2].at(b, 16 * (s // 2 + 1)))
                        nc.scalar.activation(sz[:, s % 2, :], sz[:, s % 2, :], ACT.Silu).then_inc(s_sz.sem, 1)
                    t = s - 1
                    if t >= 0:
                        act.wait_ge(*s_ygt.at(b, t + 1))
                        if t >= 2:
                            act.wait_ge(*s_o.at(b, t - 1))
                        nc.scalar.activation(ygT[:, t % 2, :, :].rearrange("p k c -> p (k c)"), banks(2 * (t % 2)), ACT.Copy
                                             ).then_inc(s_yge.sem, 1)
                    if s == 5:
                        root(n0, b + 1)

        @block.vector
        def _(dve):
            v = nc.vector
            dve.sem_inc(s_h.sem, s_h.first)
            dve.sem_inc(s_acc.sem, s_acc.first)
            dve.sem_inc(s_yg.sem, s_yg.first)
            dve.sem_inc(s_og.sem, s_og.first)
            dve.wait_ge(s_er.sem, 1)
            v.tensor_tensor(erow, ps[0:B, 0:5, :].rearrange("p a c -> p (a c)"), ebias, ALU.add).then_inc(s_erb.sem, 1)
            dve.wait_ge(s_ec.sem, 1)
            v.tensor_copy(ecol.rearrange("p s k b -> p (s k b)"), ps[:, 5, 0:4 * KD * B]).then_inc(s_pro.sem, 1)
            dve.wait_ge(s_pro.sem, 1)
            at = 1
            for scale_i, shift_i, w, bb_, gain, shift in ((0, 1, "sw", "sb", gain0, shift0), (3, 2, "lg", "lb", gain1, shift1)):
                def by_b(a):
                    return a[:, :].rearrange("p (b k) -> p k b", k=KD)

                def chan(name):
                    return col(name, 0, KD).unsqueeze(2).to_broadcast([P, KD, B])

                v.tensor_scalar_add(one_plus, ecol[:, scale_i], 1.0).then_inc(s_pro.sem, 1)
                dve.wait_ge(s_pro.sem, at + 1)
                v.tensor_tensor(by_b(gain), one_plus, chan(w), ALU.mult).then_inc(s_pro.sem, 1)
                v.tensor_tensor(prod, one_plus, chan(bb_), ALU.mult).then_inc(s_pro.sem, 1)
                dve.wait_ge(s_pro.sem, at + 3)
                v.tensor_tensor(by_b(shift), prod, ecol[:, shift_i], ALU.add).then_inc(s_pro.sem, 1)
                dve.wait_ge(s_pro.sem, at + 4)
                at += 4
            dve.wait_ge(s_ea.sem, 1)
            v.tensor_scalar_mul(negA[:, :], negA[:, :], -1.0).then_inc(s_pro.sem, 1)
            assert at + 1 == PRO
            dve.wait_ge(s_pro.sem, PRO)

            def row_stats(N, src, n):
                v.bn_stats(stats[:, n, :], src[:, n, :]).then_inc(N.stats.sem, 1)

            def inverse_var(N, b, hf):
                rows = slice(hf * HALF, (hf + 1) * HALF)
                for n in range(hf * HALF, (hf + 1) * HALF):
                    dve.wait_ge(*N.stats.at(b, n + 1))
                    dve.nop(nofuse=True)
                    v.bn_aggr(mv[:, n, :], stats[:, n, :]).then_inc(N.mv.sem, 1)
                dve.wait_ge(*N.mv.at(b, (hf + 1) * HALF))
                v.tensor_scalar_add(rv[:, rows], mv[:, rows, 1], EPS).then_inc(N.eps.sem, 1)
                dve.wait_ge(*N.eps.at(b, hf + 1))
                v.reciprocal(rv[:, rows], rv[:, rows]).then_inc(N.inv.sem, 1)

            def normalise(N, b, src, hf):
                rows = slice(hf * HALF, (hf + 1) * HALF)
                dve.wait_ge(*N.rstd.at(b, hf + 1))
                v.scalar_tensor_tensor(out=nmr[:, rows], in0=mv[:, rows, 0], scalar=-1.0, in1=rstd[:, rows],
                                       op0=ALU.mult, op1=ALU.mult).then_inc(N.shift.sem, 1)
                dve.wait_ge(*N.shift.at(b, hf + 1))
                for n in range(hf * HALF, (hf + 1) * HALF):
                    v.tensor_scalar(xhat[:, n, :], src[:, n, :], rstd[:, n:n + 1], nmr[:, n:n + 1],
                                    ALU.mult, ALU.add).then_inc(N.xhat.sem, 1)

            dve.wait_ge(*s_x.at(0, 16))
            for n in range(NT):
                row_stats(n0, X, n)
            for hf in range(2):
                inverse_var(n0, 0, hf)
            for hf in range(2):
                normalise(n0, 0, X, hf)
            with dve.Fori(0, B) as b:
                dve.wait_ge(*s_mask.at(b, 16))
                v.tensor_scalar(mask_add, mask_add, -1.0, BIG, ALU.add, ALU.mult).then_inc(s_madd.sem, 1)
                dve.wait_ge(*s_madd.at(b, 1))
                dve.wait_ge(*s_wvo.at(b, 64))
                dve.nop(nofuse=True)

                def low_part(g, c, bank):
                    part, name = ((q_part, "qb"), (k_part, "kb"))[c // TB]
                    cols = slice((c % TB) * 512, (c % TB + 1) * 512)
                    dve.wait_ge(*s_hi.at(b, g * CHUNKS + c + 1))
                    v.scalar_tensor_tensor(out=part[1][:, cols].bitcast(F32R), in0=ps[:, bank, :],
                                           scalar=par[:, columns(g + COLS[name][0], 1)], in1=part[0][:, cols],
                                           op0=ALU.add, op1=ALU.subtract).then_inc(s_lo.sem, 1)

                def add_v_bias(g, bank):
                    dve.wait_ge(*s_v.at(b, g + 1))
                    v.tensor_tensor(V, banks(bank).rearrange("p (m c) -> p m c", m=NT),
                                    vb_bc[:, columns(g * P, P)].unsqueeze(1).to_broadcast([P, NT, P]), ALU.add
                                    ).then_inc(s_vev.sem, 1)

                def mask_v(g):
                    dve.wait_ge(*s_vev.at(b, g * 2 + 1))
                    v.tensor_tensor(V, V, par[:, bass.ds(b * NT + COLS["mask"][0], NT)].unsqueeze(2)
                                    .to_broadcast([P, NT, P]), ALU.mult).then_inc(s_vev.sem, 1)

                def attend_dve(g, last):
                    for s in range(M_LAG, TILES + Y_LAG):
                        t = s - M_LAG
                        if t < TILES:
                            dve.wait_ge(*s_sc.at(b, g * TILES + t + 1))
                            if t >= SR:
                                dve.wait_ge(*s_pt.at(b, g * (2 * TILES) + 2 * (t - SR + 1)))
                            dve.nop(nofuse=True)
                            v.tensor_tensor_reduce(out=S[:, t % SR, :], in0=banks(2 * (t % 2)), in1=mask_add,
                                                   scale=-1.0, scalar=3.0e38, op0=ALU.add, op1=ALU.min,
                                                   accum_out=negmax[:, t:t + 1]).then_inc(s_mx.sem, 1)
                        if s == 2:
                            add_v_bias(g, 6)
                        if s == 5:
                            mask_v(g)
                        t = s - Y_LAG
                        if t >= 0 and t % HALF == HALF - 1:
                            half = t // HALF
                            j, hf = half // 2, half % 2
                            dve.wait_ge(*s_yt.at(b, g * (2 * HG) + half + 1))
                            dve.wait_ge(*s_rd.at(b, g * (2 * HG) + half + 1))
                            v.tensor_tensor(Y[:, hf * HALF:(hf + 1) * HALF, columns(g * P + j * HD, HD)],
                                            ps[:, 6, P:2 * P]
                                            .rearrange("p (c l) -> p c l", l=HD),
                                            rden[:, t - 3:t + 1].unsqueeze(2).to_broadcast([P, HALF, HD]), ALU.mult
                                            ).then_inc(s_yn.sem, 1)
                        t = s - C_LAG
                        if 0 <= t < TILES and t % HALF == HALF - 1:
                            half = t // HALF
                            dve.wait_ge(*s_av.at(b, g * (2 * HG) + half + 1))
                            if half >= 2:
                                dve.wait_ge(*s_yt.at(b, g * (2 * HG) + half - 1))
                            v.tensor_copy(yT[:, half % 2, :], ps[:, 6, 0:P]
                                          ).then_inc(s_yc.sem, 1)
                            dve.wait_ge(*s_ex.at(b, g * TILES + t + 1))
                            v.reciprocal(rden[:, t - 3:t + 1], den[:, t - 3:t + 1]).then_inc(s_rd.sem, 1)
                        t = s - T_LAG
                        if 0 <= t < TILES:
                            dve.wait_ge(*s_pt.at(b, g * (2 * TILES) + 2 * t + 1))
                            if t % HALF == 0:
                                half = t // HALF
                                if half >= 2:
                                    dve.wait_ge(*s_av.at(b, g * (2 * HG) + half - 1))
                                elif half == 0:
                                    for r in range(2):
                                        dve.wait_ge(*s_out[r].at(b, 0))
                            c = t % HALF
                            v.tensor_copy(PT[:, (t // HALF) % 2, 0:HALF, c * P:(c + 1) * P],
                                          ps[:, 4, :].rearrange("p (m c) -> p m c", m=HALF)
                                          ).then_inc(s_pv.sem, 1)
                        if not last and chunk_out(s) is not None:
                            low_part(g + 1, chunk_out(s), 7)
                        if last and s == TILES - HALF - 1 + Y_LAG + 1:
                            dve.wait_ge(*s_yn.at(b, G * HG * 2 - 1))
                            for n in range(HALF):
                                row_stats(n1, Y, n)
                            inverse_var(n1, b, 0)

                for c in range(CHUNKS):
                    low_part(0, c, c)
                with dve.Fori(0, G - 1) as g:
                    attend_dve(g, False)
                attend_dve(G - 1, True)
                normalise(n1, b, Y, 0)
                dve.wait_ge(*s_yn.at(b, G * HG * 2))
                for n in range(HALF, NT):
                    row_stats(n1, Y, n)
                inverse_var(n1, b, 1)
                normalise(n1, b, Y, 1)
                for n in range(NT):
                    dve.wait_ge(*s_op.at(b, n + 1))
                    dve.wait_ge(*s_xob.at(b, n + 1))
                    v.tensor_tensor(X[:, n, :], ps[:, n, :], X[:, n, :], ALU.add).then_inc(s_x1.sem, 1)
                    dve.wait_ge(*s_x1.at(b, n + 1))
                    row_stats(n2, X, n)
                    if n == HALF - 1:
                        inverse_var(n2, b, 0)
                    if n == HALF:
                        normalise(n2, b, X, 0)
                inverse_var(n2, b, 1)
                normalise(n2, b, X, 1)
                v.memset(xin[:, :, 0:DC - 1], 0.0).then_inc(s_xz.sem, 1)
                for n in range(ND):
                    dve.wait_ge(*s_c0.at(b, n + 1))
                    for i in range(DC - 1):
                        if i:
                            dve.wait_ge(*s_cv.at(b, (DC - 1) * n + i))
                        v.scalar_tensor_tensor(out=cv[:, n % 2, :], in0=xin[:, n % 2, i:i + T],
                                               scalar=col("cw", n * DC + i), in1=cv[:, n % 2, :],
                                               op0=ALU.mult, op1=ALU.add).then_inc(s_cv.sem, 1)
                def clip(n):
                    dve.wait_ge(*s_dp.at(b, n + 1))
                    v.tensor_scalar(dtmp[:, n % DL, :], banks(2 * (n % DL)), col("dtb", n), 30.0,
                                    ALU.add, ALU.min).then_inc(s_dm.sem, 1)

                dve.wait_ge(*s_xpd.at(b, 32))
                for n in range(NT):
                    dve.wait_ge(*s_ut.at(b, n + 1))
                    v.tensor_tensor(acc[:, n, :], banks(4 + 2 * (n % 2)), D_bc[:, :], ALU.mult).then_inc(s_ai.sem, 1)
                    if n == 1:
                        dve.wait_ge(*s_ct.at(b, 1))
                        v.tensor_copy(C_nat[:, :, :], banks(2).rearrange("p (n c) -> p n c", n=NT)[:, :, DTR + NS:XD]
                                      ).then_inc(s_cn.sem, 1)
                        clip(0)
                    if n == 3:
                        clip(1)
                dve.wait_ge(*s_ai.at(b, NT))
                dve.wait_ge(*s_cn.at(b, 1))
                for dg in range(DG):
                    clip(dg * DL + 2)
                    clip(dg * DL + 3)

                    def dt_and_dtu(dl):
                        n = dg * DL + dl
                        dve.wait_ge(*s_dl.at(b, n + 1))
                        v.scalar_tensor_tensor(out=dT[:, dl, :], in0=banks(2 * dl), scalar=col("dtb", n),
                                               in1=dtmp[:, dl, :], op0=ALU.add, op1=ALU.max).then_inc(s_dt.sem, 1)
                        dve.wait_ge(*s_dt.at(b, n + 1))
                        v.tensor_tensor(U[:, n, :], U[:, n, :], dT[:, dl, :], ALU.mult).then_inc(s_du.sem, 1)

                    def scan(r, q, dl):
                        k = (dg * NS + r) * DL + dl
                        dve.wait_ge(*s_da.at(b, k + 1))
                        dve.wait_ge(*s_dbu.at(b, k + 1))
                        if dl == 0:
                            dve.wait_ge(*s_ht.at(b, NT * (dg * NS + r - 1)))
                        v.tensor_tensor_scan(out=hs[:, q, dl, :], data0=banks(2 * (dl % 2)), data1=dbu[:, dl % 2, :],
                                             initial=0.0, op0=ALU.mult, op1=ALU.add).then_inc(s_h.sem, 1)

                    def add(r, n):
                        k = (dg * NS + r) * NT + n
                        dve.wait_ge(*s_ht.at(b, k + 1))
                        dve.wait_ge(*s_acc.at(b, k + 1 - NT))
                        part = acc[:, n, dg * 512:(dg + 1) * 512]
                        c_col = C_nat[:, n, r:r + 1] if isinstance(r, int) else C_nat[:, n, bass.ds(r, 1)]
                        v.scalar_tensor_tensor(out=part, in0=ps[:, 4 + n % 3, :], scalar=c_col, in1=part,
                                               op0=ALU.mult, op1=ALU.add).then_inc(s_acc.sem, 1)

                    def scan_and_add(r, q):
                        for dl in range(DL):
                            scan(r, q, dl)
                            add(r - 1, 2 * dl)
                            add(r - 1, 2 * dl + 1)

                    dt_and_dtu(0)
                    dt_and_dtu(1)
                    scan(0, 0, 0)
                    dt_and_dtu(2)
                    scan(0, 0, 1)
                    dt_and_dtu(3)
                    scan(0, 0, 2)
                    scan(0, 0, 3)
                    with dve.Fori(0, NS // 2 - 1) as i:
                        scan_and_add(i * 2 + 1, 1)
                        scan_and_add(i * 2 + 2, 0)
                    scan_and_add(NS - 1, 1)
                    for n in range(NT):
                        add(NS - 1, n)
                        if dg + 1 < DG and n in (4, 7):
                            clip((dg + 1) * DL + (n == 7))
                dve.wait_ge(*s_acc.at(b, DG * NS * NT))
                dve.wait_ge(*s_gbc.at(b, 16))
                for s in range(NT + 2):
                    if s < NT:
                        dve.wait_ge(*s_sz.at(b, s + 1))
                        v.tensor_tensor(acc[:, s, :], acc[:, s, :], sz[:, s % 2, :], ALU.mult).then_inc(s_yg.sem, 1)
                    t = s - 2
                    if t >= 0:
                        dve.wait_ge(*s_o.at(b, t + 1))
                        if t >= 2:
                            dve.wait_ge(*s_out[t % 2].at(b, 16 * (t // 2)))
                        v.tensor_tensor(res[:, t % 2, :], ps[:, 6 + t % 2, :], gate_bc, ALU.mult
                                        ).then_inc(s_og.sem, 1)
                        dve.wait_ge(*s_og.at(b, t + 1))
                        dve.wait_ge(*s_x1l[t % 2].at(b, 16 * (t // 2 + 1)))
                        v.tensor_tensor(res[:, t % 2, :], res[:, t % 2, :], x1t[:, t % 2, :], ALU.add
                                        ).then_inc(s_oa.sem, 1)
                    if s == 1:
                        dve.wait_ge(*s_x.at(b + 1, 16))
                    if 1 <= s <= HALF:
                        row_stats(n0, X, 2 * s - 2)
                        row_stats(n0, X, 2 * s - 1)
                    if s == 5:
                        inverse_var(n0, b + 1, 0)
                        inverse_var(n0, b + 1, 1)
                    if s in (6, 7):
                        normalise(n0, b + 1, X, s - 6)

        @block.tensor
        def _(pe):
            pe.sem_inc(s_qk.sem, s_qk.first)
            pe.sem_inc(s_sc.sem, s_sc.first)
            pe.sem_inc(s_ht.sem, s_ht.first)
            pe.sem_inc(s_zp.sem, s_zp.first)
            pe.sem_inc(s_o.sem, s_o.first)

            def mm(out, lhsT, rhs, k, last):
                return nc.tensor.matmul(out, lhsT, rhs, start=(k == 0), stop=(k == last))

            pe.wait_ge(s_silc.sem, 1)
            pe.wait_ge(s_emb.sem, 16 * 2 * KE)
            for k in range(KE):
                for c in range(2):
                    mm(ps[0:B, c, :], silu_c[:, k, :], emb_st[:, k, c * 512:(c + 1) * 512], k, KE - 1)
                for c in range(3):
                    last = mm(ps[0:B, 2 + c, :], silu_c[:, k, :], ada_st[k][:, c * 512:(c + 1) * 512], k, KE - 1)
            last.then_inc(s_er.sem, 1)
            pe.wait_ge(s_erb.sem, 1)
            pe.wait_ge(s_ones.sem, 4)
            for c in range(4 * KD):
                last = nc.tensor.transpose(ps[:, 5, c * B:(c + 1) * B], erow[:, c * P:(c + 1) * P], ident[0:B, 0:B])
            last.then_inc(s_ec.sem, 1)

            def norm_pe(N, b):
                for hf in range(2):
                    if hf and N is n0:
                        pe.wait_ge(*s_og.at(b, 0))
                    pe.wait_ge(*N.xhat.at(b, (hf + 1) * HALF))
                    for k in range(KD):
                        for c in range(HALF):
                            last = nc.tensor.transpose(ps[:, hf * KD + k, c * P:(c + 1) * P],
                                                       xhat[:, hf * HALF + c, k * P:(k + 1) * P], ident[:, :])
                        last.then_inc(N.tp.sem, 1)

            with pe.Fori(0, B) as b:
                norm_pe(n0, b)
                pe.wait_ge(*n0.ready.at(b, 2 * KD))
                pe.wait_ge(*s_wvo.at(b, 64))
                pe.nop(nofuse=True)

                def project_qk(c, k, bank):
                    w, th = (wq, wk)[c // TB], c % TB
                    done = mm(ps[:, bank, :], w[:, k, :], xT[:, k, th * 512:(th + 1) * 512], k, KD - 1)
                    if k == KD - 1:
                        done.then_inc(s_qk.sem, 1)

                def project_v(g, n, bank):
                    for k in range(KD):
                        done = mm(ps[:, bank + n // 4, (n % 4) * P:(n % 4 + 1) * P], xT[:, k, n * P:(n + 1) * P],
                                  wv[:, k, columns(g * P, P)], k, KD - 1)
                    if n == HALF - 1:
                        done.then_inc(s_v.sem, 1)

                def scores(g, s):
                    j, n = s // NT, s % NT
                    if s == 0:
                        pe.wait_ge(*s_lo.at(b, g * CHUNKS + CHUNKS))
                    if n == 0:
                        pe.wait_ge(*s_stk[j % 2].at(b, g * 256 + 128 * (j // 2 + 1)))
                    if s >= 2 or not isinstance(g, int) or g:
                        pe.wait_ge(*s_mx.at(b, g * TILES + s - 1))
                    for th in range(TB):
                        done = mm(ps[:, 2 * (s % 2) + th, :], q_stack[:, j % 2, n * P:(n + 1) * P],
                                  k_stack[:, j % 2, th * 512:(th + 1) * 512], 0, 0)
                    done.then_inc(s_sc.sem, 1)

                def attend_pe(g, last_group):
                    for s in range(TILES + Y_LAG):
                        if 2 <= s < TILES:
                            scores(g, s)
                        t = s - T_LAG
                        if 0 <= t < TILES:
                            pe.wait_ge(*s_ex.at(b, g * TILES + t + 1))
                            for c in range(2):
                                if t:
                                    pe.wait_ge(*(s_pa if c else s_pv).at(b, g * TILES + t))
                                for m in range(HALF):
                                    last = nc.tensor.transpose(ps[:, 4 + c, m * P:(m + 1) * P],
                                                               S[:, t % SR, (c * HALF + m) * P:(c * HALF + m + 1) * P],
                                                               ident[:, :])
                                last.then_inc(s_pt.sem, 1)
                        t = s - A_LAG
                        if HALF - 1 <= t < TILES + HALF - 1:
                            half, step = (t - HALF + 1) // HALF, (t - HALF + 1) % HALF
                            j = half // 2
                            if step == 0:
                                pe.wait_ge(*s_pv.at(b, g * TILES + (half + 1) * HALF))
                                pe.wait_ge(*s_pa.at(b, g * TILES + (half + 1) * HALF))
                                if half == 0:
                                    pe.wait_ge(*s_vev.at(b, g * 2 + 2))
                                if half >= 1:
                                    pe.wait_ge(*s_yn.at(b, g * (2 * HG) + half))
                            for m in AV_KEYS[step]:
                                for c in range(HG):
                                    last = mm(ps[c * HD:(c + 1) * HD, 6, 0:P],
                                              V[:, m, j * HD:(j + 1) * HD], PT[:, half % 2, m, c * P:(c + 1) * P],
                                              m, NT - 1)
                            if NT - 1 in AV_KEYS[step]:
                                last.then_inc(s_av.sem, 1)
                        t = s - C_LAG
                        if t >= 0 and t % HALF == HALF - 1:
                            half = t // HALF
                            pe.wait_ge(*s_yc.at(b, g * (2 * HG) + half + 1))
                            nc.tensor.transpose(ps[:, 6, P:2 * P], yT[:, half % 2, :], ident[:, :]
                                                ).then_inc(s_yt.sem, 1)
                        c, step = divmod(s - CHUNK_AT, CHUNK_STEPS)
                        if not last_group and 0 <= c < CHUNKS:
                            if c == 0 and step == 0:
                                pe.wait_ge(*s_wqk.at(b, g * 32 + 64))
                            if c and step == 0:
                                pe.wait_ge(*s_lo.at(b, (g + 1) * CHUNKS + c))
                            for k in range(KD):
                                if CHUNK_K[k] == step:
                                    project_qk(c, k, 7)
                        if not last_group and s >= Y_LAG + TILES - 3:
                            i = s - (Y_LAG + TILES - 3)
                            if i < 2:
                                scores(g + 1, i)
                            else:
                                for n in range(HALF, NT):
                                    project_v(g + 1, n, 6)
                                pe.wait_ge(*s_yn.at(b, (g + 1) * (2 * HG)))
                                for n in range(HALF):
                                    project_v(g + 1, n, 6)

                pe.wait_ge(*s_wqk.at(b, 32))
                for c in range(CHUNKS):
                    for k in range(KD):
                        project_qk(c, k, c)
                for n in range(NT):
                    project_v(0, (n + HALF) % NT, 6)
                scores(0, 0)
                scores(0, 1)
                with pe.Fori(0, G - 1) as g:
                    attend_pe(g, False)
                attend_pe(G - 1, True)
                pe.wait_ge(*s_yn.at(b, G * HG * 2))
                norm_pe(n1, b)
                for n in range(NT):
                    pe.wait_ge(*n1.ready.at(b, KD * (n // HALF + 1)))
                    for k in range(KD):
                        last = mm(ps[:, n, :], xT[:, k, n * P:(n + 1) * P], wo[:, k, :], k, KD - 1)
                    last.then_inc(s_op.sem, 1)
                norm_pe(n2, b)
                pe.wait_ge(*n2.ready.at(b, 2 * KD))
                pe.wait_ge(*s_wx.at(b, 16))
                for n in range(ND):
                    if n >= 4:
                        pe.wait_ge(*s_c0.at(b, n - 3))
                    for th in range(TB):
                        for k in range(KD):
                            last = mm(ps[:, 2 * (n % 4) + th, :], wx[:, k, n * P:(n + 1) * P],
                                      xT[:, k, th * 512:(th + 1) * 512], k, KD - 1)
                    last.then_inc(s_ip.sem, 1)
                for n in range(ND):
                    pe.wait_ge(*s_u.at(b, n + 1))
                    if n == 0:
                        pe.wait_ge(*s_c0.at(b, 5))
                        pe.wait_ge(*s_xpd.at(b, 32))
                    for th in range(TB):
                        last = mm(ps[0:XD, th, :], wxp[:, n, :], U[:, n, th * 512:(th + 1) * 512], n, ND - 1)
                last.then_inc(s_xd.sem, 1)

                def project_dt(n):
                    for th in range(TB):
                        done = mm(ps[:, 2 * (n % DL) + th, :], wdt[:, n * P:(n + 1) * P],
                                  xdT[:, th * 512:(th + 1) * 512], 0, 0)
                    done.then_inc(s_dp.sem, 1)

                for n in range(NT):
                    if n >= 2:
                        pe.wait_ge(*s_ai.at(b, n - 1))
                    for k in range(ND):
                        last = nc.tensor.transpose(ps[:, 4 + 2 * (n % 2) + k // 4, (k % 4) * P:(k % 4 + 1) * P],
                                                   U[:, k, n * P:(n + 1) * P], ident[:, :])
                    last.then_inc(s_ut.sem, 1)
                    if n == 1:
                        pe.wait_ge(*s_xde.at(b, 1))
                        for m in range(NT):
                            last = nc.tensor.transpose(ps[:, 2 + m // 4, (m % 4) * P:(m % 4 + 1) * P],
                                                       xdT[:, m * P:(m + 1) * P], ident[:, :])
                        last.then_inc(s_ct.sem, 1)
                        project_dt(0)
                    if n == 2:
                        pe.wait_ge(*s_cn.at(b, 1))
                        project_dt(1)
                pe.wait_ge(*s_ai.at(b, NT))
                for dg in range(DG):
                    if dg:
                        pe.wait_ge(*s_acc.at(b, dg * NS * NT))
                        pe.wait_ge(*s_zc.at(b, dg * NS // 2))
                    project_dt(dg * DL + 2)
                    project_dt(dg * DL + 3)
                    pe.wait_ge(*s_dt.at(b, (dg + 1) * DL))
                    if dg == 0:
                        pe.wait_ge(*s_wz.at(b, 16))
                    for r in range(dg * NS, (dg + 1) * NS):
                        pe.wait_ge(*s_h.at(b, (r + 1) * DL))
                        for n in range(NT):
                            pe.wait_ge(*s_acc.at(b, r * NT + n - (2 if n >= 3 else (1, 1, 4)[n])))
                            for dl in range(DL):
                                last = nc.tensor.transpose(ps[:, 4 + n % 3, dl * P:(dl + 1) * P],
                                                           hs[:, r % 2, dl, n * P:(n + 1) * P], ident[:, :])
                            last.then_inc(s_ht.sem, 1)
                            if n in ((3, 5), (1, 3))[r % 2]:
                                k = 2 * (r % 2) + (n >= (5, 3)[r % 2])
                                u = r // 2
                                if k == 0 and u:
                                    pe.wait_ge(*s_zc.at(b, u))
                                last = mm(ps[:, 7, :], xT[:, k, (u // 2) * P:(u // 2 + 1) * P],
                                          wz[:, k, (u % 2) * 512:(u % 2 + 1) * 512], k, KD - 1)
                                if k == KD - 1:
                                    last.then_inc(s_zp.sem, 1)
                            if r == NS - 1 and n in (2, 5):
                                project_dt(DL + (n == 5))
                pe.wait_ge(*s_acc.at(b, DG * NS * NT))
                pe.wait_ge(*s_zc.at(b, ZU))
                for s in range(NT + 1):
                    t = s
                    if t < NT:
                        pe.wait_ge(*s_yg.at(b, t + 1))
                        if t >= 2:
                            pe.wait_ge(*s_yge.at(b, t - 1))
                        for k in range(ND):
                            last = nc.tensor.transpose(ps[:, 2 * (t % 2) + k // 4, (k % 4) * P:(k % 4 + 1) * P],
                                                       acc[:, t, k * P:(k + 1) * P], ident[:, :])
                        last.then_inc(s_ygt.sem, 1)
                    t = s - 1
                    if t >= 0:
                        pe.wait_ge(*s_yge.at(b, t + 1))
                        if t == 0:
                            pe.wait_ge(*s_wp.at(b, 16))
                        if t >= 2:
                            pe.wait_ge(*s_og.at(b, t - 1))
                        for k in range(ND):
                            last = mm(ps[:, 6 + t % 2, :], ygT[:, t % 2, k, :], wp[:, k, :], k, ND - 1)
                        last.then_inc(s_o.sem, 1)
    return nc


def kernel(**inputs):
    import concourse.bacc as bacc
    from concourse.bass_utils import run_bass_kernel_spmd

    def get(name):
        return np.asarray(inputs[name])

    def cols(a):
        return a.reshape(-1, P).T

    l0, l1 = "L0_cond_", "L1_cond_"
    A_log = get(l1 + "A_log").reshape(ND, P, NS).transpose(1, 0, 2).reshape(P, ND * NS)
    conv_w = get(l1 + "conv_w").reshape(ND, P, DC).transpose(1, 0, 2).reshape(P, ND * DC)
    mask = get("mask_BxS_ff1")
    packed = {
        "nw": cols(get(l0 + "norm_w")), "nb": cols(get(l0 + "norm_b")), "qb": cols(get(l0 + "q_b")),
        "kb": cols(get(l0 + "k_b")), "sw": cols(get(l0 + "sb_norm_w")), "sb": cols(get(l0 + "sb_norm_b")),
        "lg": cols(get(l1 + "ln_g")), "lb": cols(get(l1 + "ln_b")), "cw": conv_w, "cb": cols(get(l1 + "conv_b")),
        "dtb": cols(get(l1 + "dt_proj_b")), "alog": A_log, "mask": cols(mask.reshape(-1)),
    }
    arrays = {
        "x": get("x"), "condT": get("cond_2048").T, "mask": mask,
        "params": np.concatenate([packed[name] for name in COLS], axis=1),
        "q_w": get(l0 + "q_w"), "k_w": get(l0 + "k_w"), "v_w": get(l0 + "v_w"), "v_b": get(l0 + "v_b"),
        "emb_w": get(l0 + "emb_w"), "emb_b": get(l0 + "emb_b"), "out_w": get(l0 + "out_w"), "out_b": get(l0 + "out_b"),
        "adaT": get(l1 + "ada_w").T, "ada_b": get(l1 + "ada_b"), "inT": get(l1 + "in_proj_w").T,
        "xpT": get(l1 + "x_proj_w").T, "dtT": get(l1 + "dt_proj_w").T, "D_row": get(l1 + "D_param"),
        "opT": get(l1 + "out_proj_w").T,
    }
    arrays = {name: np.ascontiguousarray(a) for name, a in arrays.items()}
    nc = bacc.Bacc("TRN2", target_bir_lowering=False, num_devices=1)
    args = [nc.dram_tensor(name, a.shape, mybir.dt.from_np(a.dtype), kind="ExternalInput").ap()
            for name, a in arrays.items()]
    args.append(nc.dram_tensor("out", (B, T, D), F32, kind="ExternalOutput").ap())
    build(nc, *args)
    r = run_bass_kernel_spmd(nc, [arrays], core_ids=[0])
    return r.results[0]["out"]
```
